# Optimizing a Trainium2 kernel written in Bass

```python
import numpy as np
import jax
import jax.numpy as jnp

def _softmax(x, axis=-1):
    return jax.nn.softmax(x, axis=axis)

def _gelu(x):
    return jax.nn.gelu(x, approximate=True)

def _silu(x):
    return jax.nn.silu(x)

def _sigmoid(x):
    return jax.nn.sigmoid(x)

def _layernorm(x, axis=-1, eps=1e-05):
    m = jnp.mean(x, axis=axis, keepdims=True)
    v = jnp.var(x, axis=axis, keepdims=True)
    return (x - m) / jnp.sqrt(v + eps)

def _scatter_add(tgt, idx, src, axis=0):
    return tgt.at[idx].add(src)

def _segment_sum(src, seg, n):
    return jax.ops.segment_sum(src, seg, n)
kernel_name = 'mk_gnn_preln_d4_gnn_r8_42e41d'

def setup_inputs(seed: int=0):
    np.random.seed(seed)
    _w = jnp.asarray

    def _rec_inputs():
        import jax
        import jax.numpy as jnp
        _gk = jax.random.key(seed)
        x = -0.000202 + 1 * jax.random.normal(jax.random.fold_in(_gk, 1), (6250, 128), jnp.float32)
        _s = jax.random.randint(jax.random.fold_in(_gk, 2), (50000,), 0, 6250, jnp.int32)
        _d = jax.random.randint(jax.random.fold_in(_gk, 3), (50000,), 0, 6250, jnp.int32)
        _loop = jnp.arange(6250, dtype=jnp.int32)
        src = jnp.concatenate([_s, _d, _loop])
        dst = jnp.concatenate([_d, _s, _loop])
        _o = jnp.argsort(dst, stable=True)
        src = src[_o]
        dst = dst[_o]
        edge_type_8 = jax.random.randint(jax.random.fold_in(_gk, 13), (106250,), 0, 8, jnp.int32)
        edge_weight = jax.random.uniform(jax.random.fold_in(_gk, 14), (106250,), jnp.float32, 0.0, 0.999998)
        node_type_4 = jax.random.randint(jax.random.fold_in(_gk, 15), (6250,), 0, 4, jnp.int32)
        return (x, src, dst, edge_type_8, edge_weight, node_type_4)
    x, src, dst, edge_type_8, edge_weight, node_type_4 = _rec_inputs()

    def _L0_gnn_setup():
        import jax, jax.numpy as jnp
        import numpy as np
        N_NODES = 6250
        N_EDGES = 100000
        IN_DIM = 128
        HID_DIM = 128
        OUT_DIM = 128

        def gcn_conv(x, W, b, src, dst, ew, n_nodes):
            h = x @ W
            deg = jax.ops.segment_sum(ew, dst, num_segments=n_nodes) + 1.0
            dis = jnp.where(deg > 0, jax.lax.rsqrt(deg), 0.0)
            norm = dis[src] * ew * dis[dst]
            msg = h[src] * norm[:, None]
            agg = jax.ops.segment_sum(msg, dst, num_segments=n_nodes)
            agg = agg + h * (dis * dis)[:, None]
            return agg + b
        key = jax.random.key(seed)
        k = jax.random.split(key, 8)
        x = jax.random.normal(k[0], (N_NODES, IN_DIM), dtype=jnp.float32)
        edge_index = jax.random.randint(k[1], (2, N_EDGES), 0, N_NODES, dtype=jnp.int64)
        edge_weight = jax.random.uniform(k[2], (N_EDGES,), dtype=jnp.float32)
        W1 = jax.random.normal(k[3], (IN_DIM, HID_DIM), dtype=jnp.float32) / np.sqrt(IN_DIM)
        b1 = jnp.zeros((HID_DIM,), dtype=jnp.float32)
        W2 = jax.random.normal(k[4], (HID_DIM, OUT_DIM), dtype=jnp.float32) / np.sqrt(HID_DIM)
        b2 = jnp.zeros((OUT_DIM,), dtype=jnp.float32)
        return {'x': x, 'edge_index': edge_index, 'edge_weight': edge_weight, 'W1': W1, 'b1': b1, 'W2': W2, 'b2': b2}
    _L0_gnn_all = _L0_gnn_setup()
    _L0_gnn_in = {k: v for k, v in _L0_gnn_all.items() if k in ('W1', 'b1', 'W2', 'b2')}
    del _L0_gnn_all

    def _L1_gnn_setup():
        import jax, jax.numpy as jnp
        import numpy as np
        import math
        HIDDEN = 128
        N_NODES = 6250
        N_EDGES = 100000
        N_NTYPES = 4
        N_ETYPES = 8

        def _type_matmul(h, W, types):
            out = jnp.zeros_like(h)
            for t in range(W.shape[0]):
                out = out + jnp.where((types == t)[:, None], h @ W[t], 0.0)
            return out

        def _sparse_softmax(scores, indices, n_segments):
            seg_max = jnp.maximum(jax.ops.segment_max(scores, indices, num_segments=n_segments), -1000000000.0)
            exp_s = jnp.exp(scores - seg_max[indices])
            seg_sum = jax.ops.segment_sum(exp_s, indices, num_segments=n_segments)
            return exp_s / (seg_sum[indices] + 1e-10)
        key = jax.random.key(seed)
        ks = jax.random.split(key, 10)
        x = jax.random.normal(ks[0], (N_NODES, HIDDEN), dtype=jnp.float32)
        edge_index = jax.random.randint(ks[1], (2, N_EDGES), 0, N_NODES, dtype=jnp.int64 if jax.config.read('jax_enable_x64') else jnp.int32)
        edge_type = jax.random.randint(ks[2], (N_EDGES,), 0, N_ETYPES, dtype=jnp.int32)
        node_type = jax.random.randint(ks[3], (N_NODES,), 0, N_NTYPES, dtype=jnp.int32)
        W_Q = jax.random.normal(ks[4], (N_NTYPES, HIDDEN, HIDDEN), dtype=jnp.float32) * 0.02
        W_K = jax.random.normal(ks[5], (N_NTYPES, HIDDEN, HIDDEN), dtype=jnp.float32) * 0.02
        W_V = jax.random.normal(ks[6], (N_NTYPES, HIDDEN, HIDDEN), dtype=jnp.float32) * 0.02
        W_edge = jax.random.normal(ks[7], (N_ETYPES, HIDDEN, HIDDEN), dtype=jnp.float32) * 0.02
        mu = jnp.ones((N_ETYPES,), dtype=jnp.float32)
        return {'x': x, 'edge_index': edge_index, 'edge_type': edge_type, 'node_type': node_type, 'W_Q': W_Q, 'W_K': W_K, 'W_V': W_V, 'W_edge': W_edge, 'mu': mu}
    _L1_gnn_all = _L1_gnn_setup()
    _L1_gnn_in = {k: v for k, v in _L1_gnn_all.items() if k in ('W_Q', 'W_K', 'W_V', 'W_edge', 'mu')}
    del _L1_gnn_all

    def _L2_gnn_setup():
        import jax, jax.numpy as jnp
        import numpy as np
        N_NODES = 6250
        N_EDGES = 100000
        D_IN = 128
        D_OUT = 128
        key = jax.random.key(seed)
        k_x, k_e, k_w, k_b = jax.random.split(key, 4)
        x = jax.random.normal(k_x, (N_NODES, D_IN), dtype=jnp.float32)
        edge_index = jax.random.randint(k_e, (2, N_EDGES), 0, N_NODES, dtype=jnp.int64)
        scale = 1.0 / np.sqrt(D_IN)
        weight = jax.random.uniform(k_w, (D_OUT, D_IN), dtype=jnp.float32, minval=-scale, maxval=scale)
        bias = jax.random.uniform(k_b, (D_OUT,), dtype=jnp.float32, minval=-scale, maxval=scale)
        return {'x': x, 'edge_index': edge_index, 'weight': weight, 'bias': bias}
    _L2_gnn_all = _L2_gnn_setup()
    _L2_gnn_in = {k: v for k, v in _L2_gnn_all.items() if k in ('weight', 'bias')}
    del _L2_gnn_all

    def _L3_gnn_setup():
        import jax, jax.numpy as jnp
        import numpy as np
        N = 5000
        DEG = 16
        E = N * DEG
        DIN = 128
        H = 8
        D = DIN // H
        FF = 4 * DIN
        HOPS = 5
        ALPHA = 0.15
        EPS = 1e-05

        def _ln(x, g, b):
            m = jnp.mean(x, axis=-1, keepdims=True)
            v = jnp.mean((x - m) ** 2, axis=-1, keepdims=True)
            return (x - m) / jnp.sqrt(v + EPS) * g + b
        key = jax.random.key(seed)
        ks = jax.random.split(key, 12)
        s = 0.05
        feat = jax.random.normal(ks[0], (N, DIN), dtype=jnp.float32)
        src = jax.random.randint(ks[1], (E,), 0, N, dtype=jnp.int32)
        dst = jnp.repeat(jnp.arange(N, dtype=jnp.int32), DEG)
        return {'feat': feat, 'Wh': jax.random.normal(ks[2], (DIN, DIN), dtype=jnp.float32) * s, 'Wt': jax.random.normal(ks[3], (DIN, DIN), dtype=jnp.float32) * s, 'We': jax.random.normal(ks[4], (DIN, DIN), dtype=jnp.float32) * s, 'attn_p': jax.random.normal(ks[5], (H, D), dtype=jnp.float32) * s, 'g_head': jax.random.normal(ks[6], (H, D), dtype=jnp.float32) * s, 'g_tail': jax.random.normal(ks[7], (H, D), dtype=jnp.float32) * s, 'ln1_g': jnp.ones((DIN,), jnp.float32), 'ln1_b': jnp.zeros((DIN,), jnp.float32), 'ln2_g': jnp.ones((DIN,), jnp.float32), 'ln2_b': jnp.zeros((DIN,), jnp.float32), 'W1': jax.random.normal(ks[8], (FF, DIN), dtype=jnp.float32) * s, 'b1': jnp.zeros((FF,), jnp.float32), 'W2': jax.random.normal(ks[9], (DIN, FF), dtype=jnp.float32) * s, 'b2': jnp.zeros((DIN,), jnp.float32), 'src': src, 'dst': dst}
    _L3_gnn_all = _L3_gnn_setup()
    _L3_gnn_in = {k: v for k, v in _L3_gnn_all.items() if k in ('Wh', 'Wt', 'We', 'attn_p', 'g_head', 'g_tail', 'ln1_g', 'ln1_b', 'ln2_g', 'ln2_b', 'W1', 'b1', 'W2', 'b2')}
    del _L3_gnn_all
    return {'x': x, 'src': src, 'dst': dst, 'edge_type_8': edge_type_8, 'edge_weight': edge_weight, 'node_type_4': node_type_4, 'L0_gnn_W1': _L0_gnn_in['W1'], 'L0_gnn_b1': _L0_gnn_in['b1'], 'L0_gnn_W2': _L0_gnn_in['W2'], 'L0_gnn_b2': _L0_gnn_in['b2'], 'L1_gnn_W_Q': _L1_gnn_in['W_Q'], 'L1_gnn_W_K': _L1_gnn_in['W_K'], 'L1_gnn_W_V': _L1_gnn_in['W_V'], 'L1_gnn_W_edge': _L1_gnn_in['W_edge'], 'L1_gnn_mu': _L1_gnn_in['mu'], 'L2_gnn_weight': _L2_gnn_in['weight'], 'L2_gnn_bias': _L2_gnn_in['bias'], 'L3_gnn_Wh': _L3_gnn_in['Wh'], 'L3_gnn_Wt': _L3_gnn_in['Wt'], 'L3_gnn_We': _L3_gnn_in['We'], 'L3_gnn_attn_p': _L3_gnn_in['attn_p'], 'L3_gnn_g_head': _L3_gnn_in['g_head'], 'L3_gnn_g_tail': _L3_gnn_in['g_tail'], 'L3_gnn_ln1_g': _L3_gnn_in['ln1_g'], 'L3_gnn_ln1_b': _L3_gnn_in['ln1_b'], 'L3_gnn_ln2_g': _L3_gnn_in['ln2_g'], 'L3_gnn_ln2_b': _L3_gnn_in['ln2_b'], 'L3_gnn_W1': _L3_gnn_in['W1'], 'L3_gnn_b1': _L3_gnn_in['b1'], 'L3_gnn_W2': _L3_gnn_in['W2'], 'L3_gnn_b2': _L3_gnn_in['b2']}

def reference(x, src, dst, edge_type_8, edge_weight, node_type_4, L0_gnn_W1, L0_gnn_b1, L0_gnn_W2, L0_gnn_b2, L1_gnn_W_Q, L1_gnn_W_K, L1_gnn_W_V, L1_gnn_W_edge, L1_gnn_mu, L2_gnn_weight, L2_gnn_bias, L3_gnn_Wh, L3_gnn_Wt, L3_gnn_We, L3_gnn_attn_p, L3_gnn_g_head, L3_gnn_g_tail, L3_gnn_ln1_g, L3_gnn_ln1_b, L3_gnn_ln2_g, L3_gnn_ln2_b, L3_gnn_W1, L3_gnn_b1, L3_gnn_W2, L3_gnn_b2):
    import jax
    import jax.numpy as jnp

    def _L0_gnn_ref(x, edge_index, edge_weight, W1, b1, W2, b2):
        import jax, jax.numpy as jnp
        import numpy as np
        N_NODES = 6250
        N_EDGES = 100000
        IN_DIM = 128
        HID_DIM = 128
        OUT_DIM = 128

        def gcn_conv(x, W, b, src, dst, ew, n_nodes):
            h = x @ W
            deg = jax.ops.segment_sum(ew, dst, num_segments=n_nodes) + 1.0
            dis = jnp.where(deg > 0, jax.lax.rsqrt(deg), 0.0)
            norm = dis[src] * ew * dis[dst]
            msg = h[src] * norm[:, None]
            agg = jax.ops.segment_sum(msg, dst, num_segments=n_nodes)
            agg = agg + h * (dis * dis)[:, None]
            return agg + b
        src, dst = (edge_index[0], edge_index[1])
        n = x.shape[0]
        h = gcn_conv(x, W1, b1, src, dst, edge_weight, n)
        h = jax.nn.relu(h)
        out = gcn_conv(h, W2, b2, src, dst, edge_weight, n)
        return out

    def _L1_gnn_ref(x, edge_index, edge_type, node_type, W_Q, W_K, W_V, W_edge, mu):
        import jax, jax.numpy as jnp
        import numpy as np
        import math
        HIDDEN = 128
        N_NODES = 6250
        N_EDGES = 100000
        N_NTYPES = 4
        N_ETYPES = 8

        def _type_matmul(h, W, types):
            out = jnp.zeros_like(h)
            for t in range(W.shape[0]):
                out = out + jnp.where((types == t)[:, None], h @ W[t], 0.0)
            return out

        def _sparse_softmax(scores, indices, n_segments):
            seg_max = jnp.maximum(jax.ops.segment_max(scores, indices, num_segments=n_segments), -1000000000.0)
            exp_s = jnp.exp(scores - seg_max[indices])
            seg_sum = jax.ops.segment_sum(exp_s, indices, num_segments=n_segments)
            return exp_s / (seg_sum[indices] + 1e-10)
        N, d = x.shape
        scale = math.sqrt(d)
        src, dst = (edge_index[0], edge_index[1])
        Q = _type_matmul(x, W_Q, node_type)
        K = _type_matmul(x, W_K, node_type)
        V = _type_matmul(x, W_V, node_type)
        q_dst = Q[dst]
        k_src = K[src]
        k_t = _type_matmul(k_src, W_edge, edge_type)
        scores = jnp.sum(q_dst * k_t, axis=-1) / scale
        scores = scores * mu[edge_type]
        attn = _sparse_softmax(scores, dst, N)
        weighted_v = V[src] * attn[:, None]
        out = jax.ops.segment_sum(weighted_v, dst, num_segments=N)
        return out

    def _L2_gnn_ref(x, edge_index, weight, bias):
        import jax, jax.numpy as jnp
        import numpy as np
        N_NODES = 6250
        N_EDGES = 100000
        D_IN = 128
        D_OUT = 128
        N = x.shape[0]
        loop = jnp.arange(N, dtype=edge_index.dtype)
        src = jnp.concatenate([edge_index[0], loop])
        dst = jnp.concatenate([edge_index[1], loop])
        ew = jnp.ones(src.shape[0], dtype=x.dtype)
        deg = jax.ops.segment_sum(ew, dst, num_segments=N)
        deg_inv_sqrt = jnp.where(deg > 0, jax.lax.rsqrt(jnp.where(deg > 0, deg, 1.0)), 0.0)
        norm = deg_inv_sqrt[src] * deg_inv_sqrt[dst]
        h = x @ weight.T
        msg = h[src] * norm[:, None]
        out = jax.ops.segment_sum(msg, dst, num_segments=N)
        return out + bias

    def _L3_gnn_ref(feat, Wh, Wt, We, attn_p, g_head, g_tail, ln1_g, ln1_b, ln2_g, ln2_b, W1, b1, W2, b2, src, dst):
        import jax, jax.numpy as jnp
        import numpy as np
        N = 5000
        DEG = 16
        E = N * DEG
        DIN = 128
        H = 8
        D = DIN // H
        FF = 4 * DIN
        HOPS = 5
        ALPHA = 0.15
        EPS = 1e-05

        def _ln(x, g, b):
            m = jnp.mean(x, axis=-1, keepdims=True)
            v = jnp.mean((x - m) ** 2, axis=-1, keepdims=True)
            return (x - m) / jnp.sqrt(v + EPS) * g + b
        n = feat.shape[0]
        h = _ln(feat, ln1_g, ln1_b)
        fh = (h @ Wh.T).reshape(n, H, D)
        ft = (h @ Wt.T).reshape(n, H, D)
        fe = (h @ We.T).reshape(n, H, D)
        e = jnp.sum(fh[src] * ft[dst] * attn_p, axis=-1) / D
        in_deg = jax.ops.segment_sum(jnp.ones_like(dst, jnp.float32), dst, num_segments=n)
        log_in = jnp.log(in_deg)
        e = e * log_in[dst][:, None]
        gh = jnp.sum(fh * g_head, axis=-1)
        gt = jnp.sum(ft * g_tail, axis=-1)
        gate = jax.nn.sigmoid(gh[src] + gt[dst])
        mx = jax.ops.segment_max(e, dst, num_segments=n)
        tag = jnp.exp(e - mx[dst]) * gate
        ssum = jax.ops.segment_sum(tag, dst, num_segments=n)
        a = tag / ssum[dst]
        feat0 = fe
        f = feat0
        for _ in range(HOPS):
            msg = f[src] * a[..., None]
            agg = jax.ops.segment_sum(msg, dst, num_segments=n)
            f = (1.0 - ALPHA) * agg + ALPHA * feat0
        rst = (f + feat.reshape(n, H, D)).reshape(n, -1)
        x = _ln(rst, ln2_g, ln2_b)
        ff = jax.nn.relu(x @ W1.T + b1) @ W2.T + b2
        return ff + rst
    edge_index = jnp.stack([src, dst])
    h = jnp.maximum(_layernorm(x, axis=-1), 0.0)
    x = x + _L0_gnn_ref(h, edge_index, edge_weight, L0_gnn_W1, L0_gnn_b1, L0_gnn_W2, L0_gnn_b2)
    h = jnp.maximum(_layernorm(x, axis=-1), 0.0)
    x = x + _L1_gnn_ref(h, edge_index, edge_type_8, node_type_4, L1_gnn_W_Q, L1_gnn_W_K, L1_gnn_W_V, L1_gnn_W_edge, L1_gnn_mu)
    h = jnp.maximum(_layernorm(x, axis=-1), 0.0)
    x = x + _L2_gnn_ref(h, edge_index, L2_gnn_weight, L2_gnn_bias)
    h = jnp.maximum(_layernorm(x, axis=-1), 0.0)
    x = x + _L3_gnn_ref(h, L3_gnn_Wh, L3_gnn_Wt, L3_gnn_We, L3_gnn_attn_p, L3_gnn_g_head, L3_gnn_g_tail, L3_gnn_ln1_g, L3_gnn_ln1_b, L3_gnn_ln2_g, L3_gnn_ln2_b, L3_gnn_W1, L3_gnn_b1, L3_gnn_W2, L3_gnn_b2, src, dst)
    return x

_drawn_inputs = setup_inputs


def setup_inputs(seed=0):
    import zlib

    import numpy as np

    out = dict(_drawn_inputs(seed))
    spreads = {'L0_gnn_b1': (0.0, 0.1),
     'L0_gnn_b2': (0.0, 0.1),
     'L1_gnn_mu': (1.0, 0.6),
     'L3_gnn_ln1_g': (1.0, 0.2),
     'L3_gnn_ln1_b': (0.0, 0.1),
     'L3_gnn_ln2_g': (1.0, 0.2),
     'L3_gnn_ln2_b': (0.0, 0.31),
     'L3_gnn_b1': (0.0, 0.1),
     'L3_gnn_b2': (0.0, 0.1)}
    factors = {'L1_gnn_W_Q': 8.0,
     'L1_gnn_W_K': 8.0,
     'L1_gnn_W_edge': 8.0,
     'L3_gnn_Wh': 8.0,
     'L3_gnn_Wt': 8.0,
     'L3_gnn_attn_p': 8.0,
     'L3_gnn_g_head': 8.0,
     'L3_gnn_g_tail': 8.0}
    for name, (base, spread) in spreads.items():
        noise = np.random.default_rng([zlib.crc32(name.encode()), seed]).standard_normal(out[name].shape)
        drawn = base * np.exp(spread * noise) if base else spread * noise
        out[name] = jnp.asarray(drawn.astype(out[name].dtype))
    for name, factor in factors.items():
        out[name] = (out[name] * factor).astype(out[name].dtype)
    return out
```

```python
from contextlib import ExitStack

import concourse.bass as bass
from concourse import mybir
from concourse.alu_op_type import AluOpType as ALU

F32, I32 = mybir.dt.float32, mybir.dt.int32
ACT = mybir.ActivationFunctionType
AX = mybir.AxisListType

P = 128
N_NODES, N_EDGES = 6250, 106250
F = 128
HEADS, DH = 8, 16
NTYPES, ETYPES = 4, 8
FF = 4 * F
HOPS, ALPHA, EPS = 5, 0.15, 1e-5

NB = -(-N_NODES // P)
NPAD = NB * P
NWIN = NPAD + P
PAD_NODE = N_NODES
GT = 4
RING = 4
TURN = GT * RING
NT = -(-N_EDGES // (P * TURN)) * TURN
NG = NT // GT
TURNS = NT // TURN
AHEAD = 2
NTX = NT + AHEAD * GT
RB = -(-NT // P)
NTR = RB * P
BG = 7
NTURNS = NB // BG
BW = BG * P
FG = F + HEADS
BIG = 1e30
assert NB % BG == 0 and NTR * HEADS >= NWIN


class Env:

    phases = 0

    def tag(self, ctx):
        self.phases += 1
        self.phase_semaphores = []
        ctx.callback(self.clear_semaphores)
        return f"_{self.phases}"

    def semaphore(self, name):
        self.phase_semaphores.append(self.nc.alloc_semaphore(name))
        return self.phase_semaphores[-1]

    def clear_semaphores(self):
        self.nc.clear_and_free_semaphores(self.phase_semaphores)
        self.nc.all_engine_barrier()


def hold(engine, env, semaphore, value):
    engine.wait_ge(semaphore, value)
    engine.sem_inc(env.held, 1)


def onehot_group(nc, env, out, first_tile):
    return nc.vector.tensor_tensor(
        out, env.iota[:, :].unsqueeze(1).to_broadcast([P, GT, P]),
        env.dloc[:, bass.ds(first_tile, GT)].unsqueeze(2).to_broadcast([P, GT, P]), ALU.is_equal)


def window_starts(nc, engine, env, first_tile):
    _, starts = nc.values_load_multi_w_load_instructions(
        env.starts[0:1, bass.ds(first_tile, GT)], engines=(engine,), min_val=0, max_val=N_NODES)
    return starts


def turns(engine, count, body):
    with engine.Fori(0, count - 1) as turn:
        body(turn, False)
    body(count - 1, True)


def load_phase(nc, env):
    with ExitStack() as ctx:
        tag = env.tag(ctx)

        def sb(name, shape, dt=F32):
            return ctx.enter_context(nc.sbuf_tensor(name + tag, shape, dt))

        def sem(name):
            return env.semaphore(name + tag)

        dst_tiles = sb("dst_tiles", [P, NT], I32)
        starts_all = sb("starts_all", [P, NT], I32)
        iota_i = sb("iota_i", [P, P], I32)
        etype = sb("etype", [P, NT], I32)
        src_lin = sb("src_lin", [P, NT], I32)
        kidx = sb("kidx", [P, NT], I32)
        ntype = sb("ntype", [P, NB], I32)
        vecs = sb("vecs", [P, 3, F])
        rowdst = sb("rowdst", [P, RB, P], I32)
        loaded, cleared, ident0, made = sem("loaded"), sem("cleared"), sem("ident0"), sem("made")
        kidx_made, kidx_stored = sem("kidx_made"), sem("kidx_stored")
        vec_done = sem("vec_done")
        zero_stored = sem("zero_stored")
        block = ctx.enter_context(nc.Block())
        I = env.ins
        loads = [
            (dst_tiles[:, :], I["dst_tiles"]),
            (starts_all[:, :], I["starts"].to_broadcast([P, NT])),
            (env.starts[0:1, 0:NT], I["starts"]),
            (src_lin[:, :], I["src_groups"].rearrange("g p u -> (g p u)").rearrange("(a b) -> a b", a=P)),
            (etype[:, :], I["etype_groups"].rearrange("g p u -> (g p u)").rearrange("(a b) -> a b", a=P)),
            (ntype[:, :], I["ntype"]),
            (env.eweight[:, 0:NT], I["eweight"]),
            (env.X[:, :, :], I["x"].rearrange("(b p) f -> p b f", p=P)),
            (rowdst[:, :, :], I["dst_rows"]),
            (env.L0W1[:, :], I["L0_gnn_W1"]), (env.L0W2[:, :], I["L0_gnn_W2"]), (env.L2W[:, :], I["L2_WT"]),
            (env.WQKV[:, :, 0:F], I["L1_gnn_W_Q"].rearrange("t i o -> i t o")),
            (env.WQKV[:, :, F:2 * F], I["L1_gnn_W_K"].rearrange("t i o -> i t o")),
            (env.WQKV[:, :, 2 * F:3 * F], I["L1_gnn_W_V"].rearrange("t i o -> i t o")),
            (env.WE[:, :, :], I["L1_gnn_W_edge"].rearrange("t i o -> i t o")),
            (env.mu[:, :], I["L1_gnn_mu"].unsqueeze(0).to_broadcast([P, ETYPES])),
            (env.W3[:, 0:F], I["L3_WhT"]), (env.W3[:, FG:FG + F], I["L3_WtT"]),
            (env.W3[:, 2 * FG:2 * FG + F], I["L3_WeT"]),
            (env.FW1[:, :], I["L3_W1T"]), (env.FW2[:, :, :], I["L3_W2T"].rearrange("(c p) o -> p c o", p=P)),
            (env.fb1[:, :], I["L3_b1"]),
        ]
        loads += [(env.rows[:, n, :], I[name].unsqueeze(0).to_broadcast([P, F])) for n, name in enumerate(env.row_names)]
        loads += [(vecs[:, n, :], I[name].unsqueeze(0).to_broadcast([P, F]))
                  for n, name in enumerate(("L3_attn", "L3_ghead", "L3_gtail"))]

        @block.sync
        def _(sp):
            for out, in_ in loads:
                sp.dma_start(out, in_).then_inc(loaded, 16)
            sp.wait_ge(kidx_made, 1)
            sp.dma_start(env.kidx_groups.rearrange("g p u -> (g p u)").rearrange("(a b) -> a b", a=P),
                         kidx[:, :]).then_inc(kidx_stored, 16)
            sp.wait_ge(cleared, 2)
            sp.dma_start(env.Qtab[NPAD:NWIN, :], env.acc[:, 0:F]).then_inc(zero_stored, 16)
            sp.dma_start(env.Dtab[NPAD:NWIN, :], env.acc[:, 0:FG]).then_inc(zero_stored, 16)
            sp.wait_ge(kidx_stored, 16)
            sp.wait_ge(zero_stored, 32)

        @block.gpsimd
        def _(pool):
            pool.memset(env.ident[:, :], 0.0).then_inc(ident0, 1)
            pool.iota(iota_i[:, :], pattern=[[1, P]], base=0, channel_multiplier=0).then_inc(made, 1)
            pool.wait_ge(ident0, 1)
            pool.affine_select(out=env.ident[:, :], in_=env.ident[:, :], compare_op=ALU.not_equal, fill=1.0,
                               base=0, pattern=[[-1, P]], channel_multiplier=1).then_inc(made, 1)

        @block.vector
        def _(dve):
            V = nc.vector
            done = [0]

            def link(ins):
                done[0] += 1
                ins.then_inc(vec_done, 1)
                dve.wait_ge(vec_done, done[0])

            V.memset(env.dloc[:, :], 0.0).then_inc(cleared, 1)
            V.memset(env.acc[:, :], 0.0).then_inc(cleared, 1)
            V.memset(env.SC[:, :], 0.0)
            V.memset(env.W[:, :], 0.0)
            link(V.memset(env.eweight[:, NT:NTX], 0.0))
            dve.wait_ge(loaded, 16 * len(loads))
            dve.wait_ge(made, 2)
            V.tensor_copy(env.iota[:, :], iota_i[:, :])
            V.tensor_tensor(env.dloc[:, 0:NT], dst_tiles[:, :], starts_all[:, :], ALU.subtract)
            V.tensor_copy(env.rowdstf[:, :, :], rowdst[:, :, :])
            V.scalar_tensor_tensor(out=kidx[:, :], in0=src_lin[:, :], scalar=float(ETYPES), in1=etype[:, :],
                                   op0=ALU.mult, op1=ALU.add).then_inc(kidx_made, 1)
            for t in range(NTYPES):
                V.tensor_scalar(env.nmask[:, :, t], ntype[:, :], float(t), None, ALU.is_equal)
            link(V.tensor_scalar(env.mu[:, :], env.mu[:, :], float(F) ** -0.5, None, ALU.mult))
            V.tensor_tensor(env.WE[:, :, :], env.WE[:, :, :],
                            env.mu[:, :].unsqueeze(2).to_broadcast([P, ETYPES, F]), ALU.mult)
            tmp = env.acc[:, NWIN - 3 * F:NWIN]
            link(V.tensor_tensor(tmp[:, F:2 * F], env.W3[:, 0:F], vecs[:, 1, :], ALU.mult))
            link(V.tensor_tensor(tmp[:, 2 * F:3 * F], env.W3[:, FG:FG + F], vecs[:, 2, :], ALU.mult))
            V.tensor_reduce(env.W3[:, F:FG], tmp[:, F:2 * F].rearrange("p (h d) -> p h d", h=HEADS), AX.X, ALU.add)
            V.tensor_reduce(env.W3[:, FG + F:2 * FG], tmp[:, 2 * F:3 * F].rearrange("p (h d) -> p h d", h=HEADS),
                            AX.X, ALU.add)
            link(V.tensor_scalar(vecs[:, 0, :], vecs[:, 0, :], 1.0 / DH, None, ALU.mult))
            link(V.tensor_tensor(env.W3[:, FG:FG + F], env.W3[:, FG:FG + F], vecs[:, 0, :], ALU.mult))


def aggregate_phase(nc, env, table, scale, heads, clear):
    with ExitStack() as ctx:
        tag = env.tag(ctx)

        def sb(name, shape, dt=F32):
            return ctx.enter_context(nc.sbuf_tensor(name + tag, shape, dt))

        def sem(name):
            return env.semaphore(name + tag)

        rows = sb("rows", [P, RING, GT, F])
        idx = sb("idx", [P, RING, GT], I32)
        onehot = sb("onehot", [P, RING, GT, P])
        wcols = sb("wcols", [P, RING, GT, max(heads, 1)])
        ready_mark = sb("ready_mark", [P, 1])
        sums = ctx.enter_context(nc.psum_tensor("sums" + tag, [P, 2, GT, P], F32))
        wsums = ctx.enter_context(nc.psum_tensor("wsums" + tag, [P, 2, GT, P], F32))
        idx_loaded = [sem(f"idx_loaded{k}") for k in range(RING)]
        gathered = [sem(f"gathered{k}") for k in range(RING)]
        scaled, staged, built, summed, added, zeroed = (sem(n) for n in (
            "scaled", "staged", "built", "summed", "added", "zeroed"))
        block = ctx.enter_context(nc.Block())

        if table is not None:
            @block.sync
            def _(sp):
                def body(turn, last):
                    for k in range(RING):
                        g = turn * RING + k
                        sp.wait_ge(summed, g + 1)
                        sp.dma_start(idx[:, k, :], env.src_groups[bass.ds(g, 1), :, :].rearrange("a p u -> (a p) u")
                                     ).then_inc(idx_loaded[k], 16)
                turns(sp, TURNS, body)

            @block.gpsimd
            def _(pool):
                def body(turn, last):
                    for k in range(RING):
                        pool.wait_ge(summed, turn * RING + k + 1)
                        hold(pool, env, idx_loaded[k], turn * 16 + 16)
                        for u in range(GT):
                            nc.gpsimd.indirect_dma_start(
                                rows[:, k, u, :], None, table,
                                bass.IndirectOffsetOnAxis(ap=idx[:, k, u:u + 1], axis=0)).then_inc(gathered[k], 16)
                turns(pool, TURNS, body)

        if heads or scale == "edge":
            @block.scalar
            def _(act):
                def body(turn, last):
                    for k in range(RING):
                        g = turn * RING + k
                        t = g * GT
                        if heads:
                            hold(act, env, summed, g + 1)
                            nc.scalar.copy(wcols[:, k, :, :], env.W[:, bass.ds(t * heads, GT * heads)].rearrange(
                                "p (u h) -> p u h", u=GT)).then_inc(staged, 1)
                        if scale == "edge":
                            hold(act, env, gathered[k], turn * 16 * GT + 16 * GT)
                            for u in range(GT):
                                last_scale = nc.scalar.activation(rows[:, k, u, :], rows[:, k, u, :], ACT.Copy,
                                                                  scale=env.edge_scale[:, bass.ds(t + u, 1)])
                            last_scale.then_inc(scaled, 1)
                turns(act, TURNS, body)

        @block.tensor
        def _(pe):
            pe.sem_inc(summed, RING)

            def body(turn, last):
                for k in range(RING):
                    g = turn * RING + k
                    pe.wait_ge(built, g + 1)
                    pe.wait_ge(added, g * GT + GT)
                    if heads:
                        pe.wait_ge(staged, g + 1)
                        for u in range(GT):
                            ins = nc.tensor.matmul(wsums[0:heads, k % 2, u, :], lhsT=wcols[:, k, u, 0:heads],
                                                   rhs=onehot[:, k, u, :], start=True, stop=True)
                    if table is not None:
                        if scale is None:
                            pe.wait_ge(gathered[k], turn * 16 * GT + 16 * GT)
                        else:
                            pe.wait_ge(scaled, g + 1)
                        for u in range(GT):
                            ins = nc.tensor.matmul(sums[:, k % 2, u, :], lhsT=rows[:, k, u, :],
                                                   rhs=onehot[:, k, u, :], start=True, stop=True)
                    ins.then_inc(summed, 1)
            turns(pe, TURNS, body)

        @block.vector
        def _(dve):
            def build(g, k):
                onehot_group(nc, env, onehot[:, k, :, :], g * GT).then_inc(built, 1)

            def scale_rows(turn, k):
                g = turn * RING + k
                dve.wait_ge(gathered[k], turn * 16 * GT + 16 * GT)
                v = rows[:, k, :, :].rearrange("p u (h d) -> p (u h) d", d=DH)
                w = env.W[:, bass.ds(g * GT * HEADS, GT * HEADS)].unsqueeze(2).to_broadcast([P, GT * HEADS, DH])
                nc.vector.tensor_tensor(v, v, w, ALU.mult).then_inc(scaled, 1)

            if clear:
                nc.vector.memset(env.acc[:, 0:NWIN], 0.0)
            if heads:
                nc.vector.memset(env.den[:, 0:NWIN], 0.0)
            nc.vector.memset(ready_mark[:, :], 0.0).then_inc(added, 2 * GT)
            for g in range(AHEAD):
                build(g, g)
            if scale == "heads":
                scale_rows(0, 0)

            def body(turn, last):
                for k in range(RING):
                    g = turn * RING + k
                    if scale == "heads" and not (last and k == RING - 1):
                        scale_rows(turn + (k + 1) // RING, (k + 1) % RING)
                    starts = window_starts(nc, mybir.EngineType.DVE, env, g * GT)
                    dve.wait_ge(summed, g + RING + 1)
                    for u in range(GT):
                        dve.wait_ge(added, g * GT + u + 2 * GT)
                        if heads:
                            d = env.den[0:heads, bass.ds(starts[u], P)]
                            ins = nc.vector.tensor_tensor(d, d, wsums[0:heads, k % 2, u, :], ALU.add)
                        if table is not None:
                            a = env.acc[:, bass.ds(starts[u], P)]
                            ins = nc.vector.tensor_tensor(a, a, sums[:, k % 2, u, :], ALU.add)
                        ins.then_inc(added, 1)
                    if not (last and k >= RING - AHEAD):
                        build(g + AHEAD, (k + AHEAD) % RING)
            turns(dve, TURNS, body)


def score_phase(nc, env, table, index_groups, windows, heads, width):
    with ExitStack() as ctx:
        tag = env.tag(ctx)

        def sb(name, shape, dt=F32):
            return ctx.enter_context(nc.sbuf_tensor(name + tag, shape, dt))

        def sem(name):
            return env.semaphore(name + tag)

        rows = sb("rows", [P, RING, GT, width])
        idx = sb("idx", [P, RING, GT], I32)
        onehot = sb("onehot", [P, RING, GT, P])
        win = sb("win", [P, RING, GT, width])
        spread = sb("spread", [P, 2, GT, P])
        prod = sb("prod", [P, 2, GT, F])
        flip = ctx.enter_context(nc.psum_tensor("flip" + tag, [P, 2, GT, P], F32))
        want = ctx.enter_context(nc.psum_tensor("want" + tag, [P, 2, GT, 2 * P], F32))
        idx_loaded = [sem(f"idx_loaded{k}") for k in range(RING)]
        gathered = [sem(f"gathered{k}") for k in range(RING)]
        win_loaded = [sem(f"win_loaded{k}") for k in range(RING)]
        built, flipped, spread_ready, wanted, multiplied, scored = (sem(n) for n in (
            "built", "flipped", "spread_ready", "wanted", "multiplied", "scored"))
        block = ctx.enter_context(nc.Block())

        @block.sync
        def _(sp):
            def body(turn, last):
                for k in range(RING):
                    g = turn * RING + k
                    sp.wait_ge(scored, g + 1)
                    sp.dma_start(idx[:, k, :], index_groups[bass.ds(g, 1), :, :].rearrange("a p u -> (a p) u")
                                 ).then_inc(idx_loaded[k], 16)
                    starts = window_starts(nc, mybir.EngineType.SP, env, g * GT)
                    for u in range(GT):
                        sp.dma_start(win[:, k, u, :], windows[bass.ds(starts[u], P), :]).then_inc(win_loaded[k], 16)
            turns(sp, TURNS, body)

        @block.gpsimd
        def _(pool):
            def body(turn, last):
                for k in range(RING):
                    pool.wait_ge(scored, turn * RING + k + 1)
                    hold(pool, env, idx_loaded[k], turn * 16 + 16)
                    for u in range(GT):
                        nc.gpsimd.indirect_dma_start(
                            rows[:, k, u, :], None, table,
                            bass.IndirectOffsetOnAxis(ap=idx[:, k, u:u + 1], axis=0)).then_inc(gathered[k], 16)
            turns(pool, TURNS, body)

        @block.tensor
        def _(pe):
            def body(turn, last):
                for k in range(RING):
                    g = turn * RING + k
                    pe.wait_ge(built, g + 1)
                    pe.wait_ge(scored, g + RING - 1)
                    for u in range(GT):
                        ins = nc.tensor.transpose(flip[:, k % 2, u, :], onehot[:, k, u, :], env.ident[:, :])
                    ins.then_inc(flipped, 1)
                    pe.wait_ge(spread_ready, g + 1)
                    pe.wait_ge(win_loaded[k], turn * 16 * GT + 16 * GT)
                    for u in range(GT):
                        ins = nc.tensor.matmul(want[:, k % 2, u, 0:width], lhsT=spread[:, k % 2, u, :],
                                               rhs=win[:, k, u, :], start=True, stop=True)
                    ins.then_inc(wanted, 1)
            turns(pe, TURNS, body)

        @block.scalar
        def _(act):
            def body(turn, last):
                for k in range(RING):
                    g = turn * RING + k
                    act.wait_ge(scored, g + RING - 1)
                    act.wait_ge(flipped, g + 1)
                    nc.scalar.copy(spread[:, k % 2, :, :], flip[:, k % 2, :, :]).then_inc(spread_ready, 1)
            turns(act, TURNS, body)

        @block.vector
        def _(dve):
            def build(g, k):
                onehot_group(nc, env, onehot[:, k, :, :], g * GT).then_inc(built, 1)

            for g in range(AHEAD):
                build(g, g)
            dve.sem_inc(scored, RING)
            score_h = env.SC[:, 0:heads * NTR].rearrange("p (h t) -> p t h", h=heads)

            def body(turn, last):
                for k in range(RING):
                    g = turn * RING + k
                    t = g * GT
                    dve.wait_ge(wanted, g + 1)
                    dve.wait_ge(gathered[k], turn * 16 * GT + 16 * GT)
                    nc.vector.tensor_tensor(prod[:, k % 2, :, :], rows[:, k, :, 0:F], want[:, k % 2, :, 0:F],
                                            ALU.mult).then_inc(multiplied, 1)
                    if width > F:
                        gate = env.W[:, bass.ds(t * HEADS, GT * HEADS)].rearrange("p (u h) -> p u h", u=GT)
                        nc.vector.tensor_tensor(gate, rows[:, k, :, F:width], want[:, k % 2, :, F:width], ALU.add)
                    if not (last and k >= RING - AHEAD):
                        build(g + AHEAD, (k + AHEAD) % RING)
                    dve.wait_ge(multiplied, g + 1)
                    nc.vector.tensor_reduce(
                        score_h[:, bass.ds(t, GT), :],
                        prod[:, k % 2, :, :].rearrange("p u (h d) -> p u h d", h=heads), AX.X, ALU.add
                    ).then_inc(scored, 1)
            turns(dve, TURNS, body)


def softmax_phase(nc, env, heads, floor, gated):
    with ExitStack() as ctx:
        tag = env.tag(ctx)

        def sb(name, shape, dt=F32):
            return ctx.enter_context(nc.sbuf_tensor(name + tag, shape, dt))

        def sem(name):
            return env.semaphore(name + tag)

        ends = sb("ends", [heads, 2, NTR])
        ends_dst = sb("ends_dst", [heads, 2, NTR], I32)
        carried = ends_dst[:, :, :].bitcast(F32)
        cont = sb("cont", [heads, NTR + 1])
        passes = sb("passes", [heads, 2, NTR])
        startflag = sb("startflag", [P, NTR + 1])
        carry = sb("carry", [P, 2, heads, RB])
        edge_of = sb("edge_of", [P, RB, P])
        bank = ctx.enter_context(nc.psum_tensor("bank" + tag, [P, 2, 4, P], F32))
        turned = ctx.enter_context(nc.psum_tensor("turned" + tag, [P, 2, 2 * 512], F32))
        ends_loaded, rowed, row_copied, maxed, end_turned, end_copied = (sem(n) for n in (
            "ends_loaded", "rowed", "row_copied", "maxed", "end_turned", "end_copied"))
        chain, carry_ready, carry_turned, shifted, unrowed, un_copied, gate_ready, exped = (sem(n) for n in (
            "chain", "carry_ready", "carry_turned", "shifted", "unrowed", "un_copied", "gate_ready", "exped"))
        block = ctx.enter_context(nc.Block())
        S_rows = env.acc[:, 0:heads * NTR].rearrange("p (h b e) -> p h b e", h=heads, b=RB)
        M_rows = env.den[:, 0:heads * NTR].rearrange("p (h b e) -> p h b e", h=heads, b=RB)
        T_rows = env.SC[:, 0:heads * NTR].rearrange("p (h b e) -> p h b e", h=heads, b=RB)
        flat_S = env.acc[:, 0:heads * NTR].rearrange("p (n e) -> p n e", e=P)
        flat_C = env.SC[:, 0:heads * NTR].rearrange("p (n e) -> p n e", e=P)
        n_sq = heads * RB
        n_batch = -(-n_sq // 4)

        @block.sync
        def _(sp):
            sp.dma_start(ends_dst[:, :, :], env.ins["dst_ends"].unsqueeze(0).to_broadcast([heads, 2, NTR])
                         ).then_inc(ends_loaded, 16)
            sp.wait_ge(ends_loaded, 16)

        @block.tensor
        def _(pe):
            for c in range(n_batch):
                if c >= 2:
                    pe.wait_ge(row_copied, c - 1)
                for s in range(4 * c, min(4 * c + 4, n_sq)):
                    ins = nc.tensor.transpose(bank[:, c % 2, s % 4, :], flat_C[:, s, :], env.ident[:, :])
                ins.then_inc(rowed, 1)
            pe.wait_ge(maxed, 1)
            for side, at in ((0, 0), (1, P - 1)):
                for b in range(RB):
                    ins = nc.tensor.transpose(turned[0:heads, side, b * P:(b + 1) * P], M_rows[:, :, b, at],
                                              env.ident[:, :])
            ins.then_inc(end_turned, 1)
            pe.wait_ge(carry_ready, 1)
            for side in range(2):
                for b in range(RB):
                    ins = nc.tensor.transpose(turned[:, side, b * heads:(b + 1) * heads],
                                              carried[:, side, b * P:(b + 1) * P], env.ident[0:heads, 0:heads])
            ins.then_inc(carry_turned, 1)
            pe.wait_ge(shifted, 1)
            pe.wait_ge(row_copied, n_batch)
            for c in range(n_batch):
                if c >= 2:
                    pe.wait_ge(un_copied, c - 1)
                for s in range(4 * c, min(4 * c + 4, n_sq)):
                    ins = nc.tensor.transpose(bank[:, c % 2, s % 4, :], flat_S[:, s, :], env.ident[:, :])
                ins.then_inc(unrowed, 1)

        @block.scalar
        def _(act):
            for c in range(n_batch):
                n = min(4, n_sq - 4 * c)
                act.wait_ge(rowed, c + 1)
                nc.scalar.copy(flat_S[:, 4 * c:4 * c + n, :], bank[:, c % 2, 0:n, :]).then_inc(row_copied, 1)
            if gated:
                nc.scalar.activation(env.W[:, :], env.W[:, :], ACT.Sigmoid).then_inc(gate_ready, 1)
            for c in range(n_batch):
                n = min(4, n_sq - 4 * c)
                act.wait_ge(unrowed, c + 1)
                nc.scalar.activation(flat_C[:, 4 * c:4 * c + n, :], bank[:, c % 2, 0:n, :], ACT.Exp
                                     ).then_inc(un_copied, 1)

        @block.vector
        def _(dve):
            V = nc.vector
            done = [0]

            def link(ins):
                done[0] += 1
                ins.then_inc(chain, 1)
                dve.wait_ge(chain, done[0])

            dve.wait_ge(ends_loaded, 16)
            V.memset(cont[:, :], -BIG)
            V.memset(startflag[:, :], -BIG)
            link(V.tensor_copy(ends[:, :, :], ends_dst[:, :, :]))
            flag = startflag[:, 0:NTR].rearrange("p (b e) -> p b e", b=RB)
            V.tensor_tensor(flag[:, :, 1:P], env.rowdstf[:, :, 1:P], env.rowdstf[:, :, 0:P - 1], ALU.is_equal)
            V.tensor_tensor(cont[:, 1:NTR], ends[:, 0, 1:NTR], ends[:, 1, 0:NTR - 1], ALU.is_equal)
            link(V.tensor_tensor(passes[:, 1, :], ends[:, 0, :], ends[:, 1, :], ALU.is_equal))
            V.tensor_scalar(flag[:, :, 1:P], flag[:, :, 1:P], -1.0, BIG, ALU.add, ALU.mult)
            V.tensor_scalar(cont[:, 1:NTR], cont[:, 1:NTR], -1.0, BIG, ALU.add, ALU.mult)
            link(V.tensor_scalar(passes[:, 1, :], passes[:, 1, :], -1.0, BIG, ALU.add, ALU.mult))
            link(V.tensor_tensor(passes[:, 0, :], passes[:, 1, :], cont[:, 0:NTR], ALU.add))
            V.tensor_tensor(passes[:, 1, :], passes[:, 1, :], cont[:, 1:NTR + 1], ALU.add)
            dve.wait_ge(row_copied, n_batch)
            for h in range(heads):
                scan = V.tensor_tensor_scan(env.den[:, h * NTR:(h + 1) * NTR], startflag[:, 0:NTR],
                                            env.acc[:, h * NTR:(h + 1) * NTR], -BIG, ALU.add, ALU.max)
            link(scan)
            for h in range(heads):
                m = env.den[:, h * NTR:(h + 1) * NTR][:, ::-1]
                scan = V.tensor_tensor_scan(m, startflag[:, 1:NTR + 1][:, ::-1], m, -BIG, ALU.add, ALU.max)
            scan.then_inc(maxed, 1)
            dve.wait_ge(end_turned, 1)
            link(V.tensor_copy(ends[:, :, :], turned[0:heads, :, 0:NTR]))
            V.tensor_tensor_scan(ends[:, 1, :], passes[:, 0, :], ends[:, 1, :], -BIG, ALU.add, ALU.max)
            back = ends[:, 0, :][:, ::-1]
            link(V.tensor_tensor_scan(back, passes[:, 1, :][:, ::-1], back, -BIG, ALU.add, ALU.max))
            V.memset(carried[:, 0, 0:1], -BIG)
            V.memset(carried[:, 1, NTR - 1:NTR], -BIG)
            V.tensor_tensor(carried[:, 0, 1:NTR], ends[:, 1, 0:NTR - 1], cont[:, 1:NTR], ALU.add)
            V.tensor_tensor(carried[:, 1, 0:NTR - 1], ends[:, 0, 1:NTR], cont[:, 1:NTR], ALU.add
                            ).then_inc(carry_ready, 1)
            dve.wait_ge(carry_turned, 1)
            for side in range(2):
                ins = V.tensor_copy(carry[:, side, :, :], turned[:, side, 0:RB * heads].rearrange(
                    "p (b h) -> p h b", b=RB))
            link(ins)
            for side in range(2):
                end = env.rowdstf[:, :, side * (P - 1):side * (P - 1) + 1].to_broadcast([P, RB, P])
                link(V.tensor_tensor(edge_of[:, :, :], env.rowdstf[:, :, :], end, ALU.is_equal))
                link(V.tensor_scalar(edge_of[:, :, :], edge_of[:, :, :], -1.0, BIG, ALU.add, ALU.mult))
                c = carry[:, side, :, :].unsqueeze(3).to_broadcast([P, heads, RB, P])
                for h in range(heads):
                    ins = V.tensor_tensor(T_rows[:, h, :, :], c[:, h, :, :], edge_of[:, :, :], ALU.add)
                link(ins)
                link(V.tensor_tensor(M_rows, M_rows, T_rows, ALU.max))
            if floor is not None:
                link(V.tensor_scalar(M_rows, M_rows, floor, None, ALU.max))
            V.tensor_tensor(S_rows, S_rows, M_rows, ALU.subtract).then_inc(shifted, 1)
            dve.wait_ge(un_copied, n_batch)
            w = env.W[:, 0:NT * heads].rearrange("p (t h) -> p t h", h=heads)
            e = env.SC[:, 0:heads * NTR].rearrange("p (h t) -> p t h", h=heads)[:, 0:NT, :]
            if gated:
                dve.wait_ge(gate_ready, 1)
                V.tensor_tensor(w, w, e, ALU.mult).then_inc(exped, 1)
            else:
                V.tensor_copy(w, e).then_inc(exped, 1)
            dve.wait_ge(exped, 1)


def turn_den_phase(nc, env, heads, finish):
    with ExitStack() as ctx:
        tag = env.tag(ctx)

        def sem(name):
            return env.semaphore(name + tag)

        nodes = ctx.enter_context(nc.sbuf_tensor("nodes" + tag, [P, NB, heads], F32))
        turned = ctx.enter_context(nc.psum_tensor("turned" + tag, [P, 512], F32))
        den_turned, chain, to_root, rooted = sem("den_turned"), sem("chain"), sem("to_root"), sem("rooted")
        block = ctx.enter_context(nc.Block())

        @block.tensor
        def _(pe):
            for b in range(NB):
                ins = nc.tensor.transpose(turned[:, b * heads:(b + 1) * heads], env.den[0:heads, b * P:(b + 1) * P],
                                          env.ident[0:heads, 0:heads])
            ins.then_inc(den_turned, 1)

        if finish == "degrees":
            @block.scalar
            def _(act):
                act.wait_ge(to_root, 1)
                nc.scalar.activation(env.dis[:, :, :], env.dis[:, :, :], ACT.Sqrt)
                nc.scalar.activation(env.logdeg[:, :], env.logdeg[:, :], ACT.Ln).then_inc(rooted, 1)

        @block.vector
        def _(dve):
            V = nc.vector
            done = [0]

            def link(ins):
                done[0] += 1
                ins.then_inc(chain, 1)
                dve.wait_ge(chain, done[0])

            dve.wait_ge(den_turned, 1)
            link(V.tensor_copy(nodes[:, :, :], turned[:, 0:NB * heads].rearrange("p (b h) -> p b h", b=NB)))
            if finish == "degrees":
                link(V.tensor_scalar(env.logdeg[:, :], nodes[:, :, 1], 1.0, None, ALU.max))
                link(V.tensor_scalar(nodes[:, :, :], nodes[:, :, :], 1.0, None, ALU.add))
                V.tensor_scalar(env.dis[:, :, :], nodes[:, :, :], 1e-30, None, ALU.max).then_inc(to_root, 1)
                dve.wait_ge(rooted, 1)
                V.tensor_scalar(nodes[:, :, :], nodes[:, :, :], 0.0, None, ALU.is_gt)
                link(V.reciprocal(env.dis[:, :, :], env.dis[:, :, :]))
                link(V.tensor_tensor(env.dis[:, :, :], env.dis[:, :, :], nodes[:, :, :], ALU.mult))
            elif finish == "attention":
                link(V.tensor_scalar(nodes[:, :, :], nodes[:, :, :], 1e-10, None, ALU.add))
                link(V.reciprocal(env.rden[:, :, 0:1], nodes[:, :, :]))
            else:
                link(V.tensor_scalar(nodes[:, :, :], nodes[:, :, :], 1e-37, None, ALU.max))
                link(V.reciprocal(env.rden[:, :, :], nodes[:, :, :]))
                link(V.tensor_scalar(env.rden[:, :, :], env.rden[:, :, :], 1.0 - ALPHA, None, ALU.mult))


class Norm:

    def __init__(self, nc, env, ctx, tag):
        self.nc = nc
        self.stats = ctx.enter_context(nc.sbuf_tensor(f"stats{tag}", [P, BG, 6], F32))
        self.mv = ctx.enter_context(nc.sbuf_tensor(f"mv{tag}", [P, BG, 2], F32))
        self.root = ctx.enter_context(nc.sbuf_tensor(f"root{tag}", [P, BG], F32))
        self.rstd = ctx.enter_context(nc.sbuf_tensor(f"rstd{tag}", [P, BG], F32))
        self.shift = ctx.enter_context(nc.sbuf_tensor(f"shift{tag}", [P, BG], F32))
        self.moments = env.semaphore(f"moments{tag}")
        self.rooted = env.semaphore(f"rooted{tag}")
        self.factors = env.semaphore(f"factors{tag}")

    def on_vector(self, dve, it, src, link):
        V = self.nc.vector
        for b in range(BG):
            ins = V.bn_stats(self.stats[:, b, :], src(b))
        link(ins)
        for b in range(BG):
            ins = V.bn_aggr(self.mv[:, b, :], self.stats[:, b, :])
        link(ins)
        V.tensor_scalar(self.root[:, :], self.mv[:, :, 1], EPS, None, ALU.add).then_inc(self.moments, 1)
        dve.wait_ge(self.rooted, it + 1)
        link(V.reciprocal(self.rstd[:, :], self.root[:, :]))
        V.scalar_tensor_tensor(out=self.shift[:, :], in0=self.mv[:, :, 0], scalar=-1.0, in1=self.rstd[:, :],
                               op0=ALU.mult, op1=ALU.mult).then_inc(self.factors, 1)

    def on_scalar(self, act, it, src, out, func):
        act.wait_ge(self.moments, it + 1)
        self.nc.scalar.activation(self.root[:, :], self.root[:, :], ACT.Sqrt).then_inc(self.rooted, 1)
        act.wait_ge(self.factors, it + 1)
        for b in range(BG):
            ins = self.nc.scalar.activation(out(b), src(b), func, bias=self.shift[:, b:b + 1],
                                            scale=self.rstd[:, b:b + 1])
        return ins


class Links:

    def __init__(self, dve, env, sem, it, steps):
        self.env = env
        self.dve, self.sem, self.steps, self.it, self.n = dve, sem, steps, it, 0

    def __call__(self, ins):
        self.n += 1
        ins.then_inc(self.sem, 1)
        hold(self.dve, self.env, self.sem, self.it * self.steps + self.n)

    def close(self):
        assert self.n == self.steps, self.n


def node_phase(nc, env, kind):
    with ExitStack() as ctx:
        tag = env.tag(ctx)

        def sb(name, shape, dt=F32):
            return ctx.enter_context(nc.sbuf_tensor(name + tag, shape, dt))

        def sem(name):
            return env.semaphore(name + tag)

        take = kind != "start"
        weight = {"conv1": env.L0W1, "conv2": env.L0W2, "conv3": env.L2W}.get(kind)
        bias = {"conv1": 0, "conv2": 1, "conv3": 2}.get(kind)
        factor = {"start": 0, "conv1": 0, "conv2": 0, "attend": 1, "conv3": 1}.get(kind)
        refill = kind in ("start", "conv1", "attend")
        staged = sb("staged", [P, BW])
        y = sb("y", [P, BG, F])
        h = sb("h", [P, BG, F])
        outrow = sb("outrow", [P, BG, F])
        feat = sb("feat", [P, BG, F])
        norm = Norm(nc, env, ctx, "_a" + tag)
        norm2 = Norm(nc, env, ctx, "_b" + tag)
        prod = ctx.enter_context(nc.psum_tensor("prod" + tag, [P, 2 * 512], F32))
        flip = ctx.enter_context(nc.psum_tensor("flip" + tag, [P, 2 * 512], F32))
        (acc_staged, product_ready, y_ready, h_ready, rows_ready, stored, flipped, refilled, chain, feat_loaded,
         turn_free) = (sem(n) for n in (
             "acc_staged", "product_ready", "y_ready", "h_ready", "rows_ready", "stored", "flipped", "refilled",
             "chain", "feat_loaded", "turn_free"))
        block = ctx.enter_context(nc.Block())
        table = {"start": env.Htab, "conv1": env.Htab, "attend": env.Htab, "hop": env.Ftab, "conv3": env.Feat}.get(kind)
        stored_rows = h if kind == "conv3" else outrow

        def table_rows(tab, it):
            return tab[bass.ds(it * BW, BW), :].rearrange("(b p) f -> p b f", p=P)

        def x_block(it, b):
            return env.X[:, bass.ds(it * BG + b, 1), :].rearrange("p a f -> p (a f)")

        @block.sync
        def _(sp):
            sp.sem_inc(turn_free, 1)
            with sp.Fori(0, NTURNS) as it:
                if kind == "last":
                    sp.wait_ge(turn_free, it + 1)
                    sp.dma_start(feat[:, :, :], table_rows(env.Feat, it)).then_inc(feat_loaded, 16)
                sp.wait_ge(rows_ready, it + 1)
                if table is not None:
                    sp.dma_start(table_rows(table, it), stored_rows[:, :, :]).then_inc(stored, 16)
                    sp.wait_ge(stored, it * 16 + 16)
                sp.sem_inc(turn_free, 1)

        if take or refill:
            @block.tensor
            def _(pe):
                with pe.Fori(0, NTURNS) as it:
                    if take:
                        pe.wait_ge(acc_staged, it + 1)
                        for b in range(BG):
                            part = staged[:, b * P:(b + 1) * P]
                            if weight is not None:
                                ins = nc.tensor.matmul(prod[:, b * P:(b + 1) * P], lhsT=part, rhs=weight[:, :],
                                                       start=True, stop=True)
                            else:
                                ins = nc.tensor.transpose(prod[:, b * P:(b + 1) * P], part, env.ident[:, :])
                        ins.then_inc(product_ready, 1)
                    if refill:
                        pe.wait_ge(refilled, it + 1)
                        pe.wait_ge(rows_ready, it + 1)
                        for b in range(BG):
                            ins = nc.tensor.transpose(flip[:, b * P:(b + 1) * P], outrow[:, b, :], env.ident[:, :])
                        ins.then_inc(flipped, 1)

        @block.scalar
        def _(act):
            act.sem_inc(refilled, 1)
            with act.Fori(0, NTURNS) as it:
                hold(act, env, turn_free, it + 1)
                if take:
                    nc.scalar.copy(staged[:, :], env.acc[:, bass.ds(it * BW, BW)]).then_inc(acc_staged, 1)
                if kind == "conv1":
                    act.wait_ge(y_ready, it + 1)
                    nc.scalar.activation(h[:, :, :], y[:, :, :], ACT.Relu).then_inc(h_ready, 1)
                elif kind == "last":
                    norm.on_scalar(act, it, lambda b: y[:, b, :], lambda b: h[:, b, :], ACT.Identity
                                   ).then_inc(h_ready, 1)
                elif kind != "hop":
                    norm.on_scalar(act, it, lambda b: x_block(it, b), lambda b: h[:, b, :], ACT.Relu
                                   ).then_inc(h_ready, 1)
                if kind == "conv3":
                    norm2.on_scalar(act, it, lambda b: h[:, b, :], lambda b: y[:, b, :], ACT.Identity
                                    ).then_inc(y_ready, 1)
                if refill:
                    hold(act, env, flipped, it + 1)
                    nc.scalar.copy(env.acc[:, bass.ds(it * BW, BW)], flip[:, 0:BW]).then_inc(refilled, 1)

        steps = {"start": 3, "conv1": 1, "conv2": 6, "attend": 5, "conv3": 10, "hop": 1, "last": 7}[kind]

        @block.vector
        def _(dve):
            V = nc.vector
            with dve.Fori(0, NTURNS) as it:
                link = Links(dve, env, chain, it, steps)
                x_turn = env.X[:, bass.ds(it * BG, BG), :]
                h_turn = env.den[:, bass.ds(it * BW, BW)].rearrange("p (b f) -> p b f", b=BG)
                f0_turn = env.SC[:, bass.ds(it * BW, BW)]
                flat_y = y[:, :, :].rearrange("p b f -> p (b f)")

                def per_node(values):
                    return values.to_broadcast([P, BG, F])

                def row(name):
                    return env.rows[:, env.row_names.index(name), :].unsqueeze(1).to_broadcast([P, BG, F])

                hold(dve, env, turn_free, it + 1)
                if take:
                    dve.wait_ge(product_ready, it + 1)
                    prod_rows = prod[:, 0:BW].rearrange("p (b f) -> p b f", b=BG)
                    if kind in ("hop", "last"):
                        r = env.rden[:, bass.ds(it * BG, BG), :].rearrange("p b h -> p (b h)").unsqueeze(
                            2).to_broadcast([P, BG * HEADS, DH])
                        link(V.tensor_tensor(y[:, :, :].rearrange("p b (h d) -> p (b h) d", h=HEADS),
                                             prod[:, 0:BW].rearrange("p (n d) -> p n d", d=DH), r, ALU.mult))
                    elif kind == "attend":
                        link(V.tensor_tensor(y[:, :, :], prod_rows, per_node(env.rden[:, bass.ds(it * BG, BG), 0:1]),
                                             ALU.mult))
                    else:
                        link(V.tensor_tensor(y[:, :, :], prod_rows,
                                             per_node(env.dis[:, bass.ds(it * BG, BG), factor:factor + 1]), ALU.mult))
                    if kind == "conv1":
                        V.tensor_tensor(y[:, :, :], y[:, :, :], row("L0_gnn_b1"), ALU.add).then_inc(y_ready, 1)
                    elif bias is not None:
                        link(V.tensor_tensor(y[:, :, :], y[:, :, :], row(env.row_names[bias]), ALU.add))
                    if kind in ("conv2", "attend", "conv3"):
                        link(V.tensor_tensor(x_turn, x_turn, y[:, :, :], ALU.add))
                if kind in ("start", "conv2", "attend", "conv3"):
                    norm.on_vector(dve, it, lambda b: x_block(it, b), link)
                    hold(dve, env, h_ready, it + 1)
                if kind == "conv1":
                    hold(dve, env, h_ready, it + 1)
                if refill:
                    V.tensor_tensor(outrow[:, :, :], h[:, :, :],
                                    per_node(env.dis[:, bass.ds(it * BG, BG), factor:factor + 1]), ALU.mult
                                    ).then_inc(rows_ready, 1)
                elif kind == "conv2":
                    V.tensor_copy(h_turn, h[:, :, :]).then_inc(rows_ready, 1)
                elif kind == "conv3":
                    norm2.on_vector(dve, it, lambda b: h[:, b, :], link)
                    dve.wait_ge(y_ready, it + 1)
                    link(V.tensor_tensor(y[:, :, :], y[:, :, :], row("L3_gnn_ln1_g"), ALU.mult))
                    V.tensor_tensor(h_turn, y[:, :, :], row("L3_gnn_ln1_b"), ALU.add).then_inc(rows_ready, 1)
                elif kind == "hop":
                    V.scalar_tensor_tensor(out=outrow[:, :, :].rearrange("p b f -> p (b f)"), in0=f0_turn,
                                           scalar=ALPHA, in1=flat_y, op0=ALU.mult, op1=ALU.add
                                           ).then_inc(rows_ready, 1)
                elif kind == "last":
                    link(V.scalar_tensor_tensor(out=flat_y, in0=f0_turn, scalar=ALPHA, in1=flat_y,
                                                op0=ALU.mult, op1=ALU.add))
                    dve.wait_ge(feat_loaded, it * 16 + 16)
                    link(V.tensor_tensor(y[:, :, :], y[:, :, :], feat[:, :, :], ALU.add))
                    V.tensor_tensor(x_turn, x_turn, y[:, :, :], ALU.add)
                    norm.on_vector(dve, it, lambda b: y[:, b, :], link)
                    hold(dve, env, h_ready, it + 1)
                    link(V.tensor_tensor(h[:, :, :], h[:, :, :], row("L3_gnn_ln2_g"), ALU.mult))
                    V.tensor_tensor(h_turn, h[:, :, :], row("L3_gnn_ln2_b"), ALU.add).then_inc(rows_ready, 1)
                link.close()


def project_phase(nc, env, kind):
    with ExitStack() as ctx:
        tag = env.tag(ctx)

        def sb(name, shape, dt=F32):
            return ctx.enter_context(nc.sbuf_tensor(name + tag, shape, dt))

        def sem(name):
            return env.semaphore(name + tag)

        att = kind == "attention"
        nm = NTYPES if att else 1
        ncol = 3 * F if att else 2 * FG + F
        masked = sb("masked", [P, 2, nm, F])
        mT = sb("mT", [P, 2, nm, P])
        outc = sb("outc", [P, 2, ncol])
        kT = sb("kT", [P, 2, P])
        ke = sb("ke", [P, 2, ETYPES * F])
        flip = ctx.enter_context(nc.psum_tensor("flip" + tag, [P, 2, 512], F32))
        proj = ctx.enter_context(nc.psum_tensor("proj" + tag, [P, 2, 512], F32))
        kflip = ctx.enter_context(nc.psum_tensor("kflip" + tag, [P, 512], F32))
        kproj = ctx.enter_context(nc.psum_tensor("kproj" + tag, [P, 2 * 512], F32))
        masked_ready, flipped, turned, projected, copied, key_flipped, key_turned, key_projected, out_ready = (
            sem(n) for n in ("masked_ready", "flipped", "turned", "projected", "copied", "key_flipped", "key_turned",
                             "key_projected", "out_ready"))
        stored = [sem("stored_even"), sem("stored_odd")]
        slot_stored = sem("slot_stored")
        block = ctx.enter_context(nc.Block())
        stores = ((env.Qtab, outc, 0, F), (env.Vtab, outc, 2 * F, 3 * F), (env.Ktab, ke, 0, ETYPES * F)) if att else (
            (env.FTtab, outc, 0, FG), (env.Dtab, outc, FG, 2 * FG), (env.FEtab, outc, 2 * FG, 2 * FG + F))

        def steps(engine, body):
            body(0, 0, 0)
            body(1, 0, 1)
            with engine.Fori(1, NB // 2) as pair:
                body(pair * 2, pair, 0)
                body(pair * 2 + 1, pair, 1)
            body(NB - 1, NB // 2, 0)

        def after(engine, semaphore, count):
            if not (isinstance(count, int) and count <= 0):
                engine.wait_ge(semaphore, count)

        @block.sync
        def _(sp):
            def body(n, pair, s):
                sp.wait_ge(out_ready, n + 1)
                for tab, src, a, b in stores:
                    sp.dma_start(tab[bass.ds(n * P, P), :], src[:, s, a:b]).then_inc(stored[s], 16)
                if s == 1:
                    sp.wait_ge(stored[0], pair * 48 + 48)
                    sp.sem_inc(slot_stored, 1)
                elif not (isinstance(pair, int) and pair == 0):
                    sp.wait_ge(stored[1], pair * 48)
                    sp.sem_inc(slot_stored, 1)
            steps(sp, body)
            sp.wait_ge(stored[0], 48 * (NB // 2 + 1))

        @block.tensor
        def _(pe):
            def body(n, pair, s):
                after(pe, turned, n - 1)
                pe.wait_ge(masked_ready, n + 1)
                for m in range(nm):
                    ins = nc.tensor.transpose(flip[:, s, m * P:(m + 1) * P], masked[:, s, m, :], env.ident[:, :])
                ins.then_inc(flipped, 1)
                after(pe, copied, n - 1)
                pe.wait_ge(turned, n + 1)
                for m in range(nm):
                    rhs = env.WQKV[:, m, :] if att else env.W3[:, :]
                    ins = nc.tensor.matmul(proj[:, s, 0:ncol], lhsT=mT[:, s, m, :], rhs=rhs, start=m == 0,
                                           stop=m == nm - 1)
                ins.then_inc(projected, 1)
                if att:
                    after(pe, key_turned, n)
                    pe.wait_ge(copied, n + 1)
                    nc.tensor.transpose(kflip[:, 0:P], outc[:, s, F:2 * F], env.ident[:, :]).then_inc(key_flipped, 1)
                    after(pe, out_ready, n)
                    pe.wait_ge(key_turned, n + 1)
                    for half in range(2):
                        types = env.WE[:, half * 4:half * 4 + 4, :].rearrange("p t f -> p (t f)")
                        ins = nc.tensor.matmul(kproj[:, half * 512:half * 512 + 512], lhsT=kT[:, s, :], rhs=types,
                                               start=True, stop=True)
                    ins.then_inc(key_projected, 1)
            steps(pe, body)

        @block.vector
        def _(dve):
            def body(n, pair, s):
                after(dve, flipped, n - 1)
                h_block = env.den[:, bass.ds(n * P, P)]
                if att:
                    kinds = env.nmask[:, bass.ds(n, 1), :].rearrange("p a t -> p (a t)")
                    nc.vector.tensor_tensor(masked[:, s, :, :], h_block.unsqueeze(1).to_broadcast([P, NTYPES, F]),
                                            kinds.unsqueeze(2).to_broadcast([P, NTYPES, F]), ALU.mult
                                            ).then_inc(masked_ready, 1)
                    dve.wait_ge(key_flipped, n + 1)
                    nc.vector.tensor_copy(kT[:, s, :], kflip[:, 0:P]).then_inc(key_turned, 1)
                    after(dve, slot_stored, n - 1)
                    dve.wait_ge(key_projected, n + 1)
                    nc.vector.tensor_copy(ke[:, s, :], kproj[:, :]).then_inc(out_ready, 1)
                else:
                    nc.vector.tensor_copy(masked[:, s, 0, :], h_block).then_inc(masked_ready, 1)
                    dve.wait_ge(copied, n + 1)
                    tail = outc[:, s, FG:FG + F]
                    nc.vector.tensor_scalar(tail, tail, env.logdeg[:, bass.ds(n, 1)], None, ALU.mult
                                            ).then_inc(out_ready, 1)
            steps(dve, body)

        @block.scalar
        def _(act):
            def body(n, pair, s):
                after(act, projected, n - 1)
                act.wait_ge(flipped, n + 1)
                nc.scalar.copy(mT[:, s, :, :].rearrange("p m f -> p (m f)"), flip[:, s, 0:nm * P]).then_inc(turned, 1)
                after(act, slot_stored, n - 1)
                act.wait_ge(projected, n + 1)
                nc.scalar.copy(outc[:, s, :], proj[:, s, 0:ncol]).then_inc(copied, 1)
            steps(act, body)


def feed_forward_phase(nc, env, out):
    with ExitStack() as ctx:
        tag = env.tag(ctx)

        def sb(name, shape, dt=F32):
            return ctx.enter_context(nc.sbuf_tensor(name + tag, shape, dt))

        def sem(name):
            return env.semaphore(name + tag)

        NC = FF // P
        h = sb("h", [P, BG, F])
        hT = sb("hT", [P, BW])
        hidden = sb("hidden", [P, NC, BW])
        y = sb("y", [P, BG, F])
        flip = ctx.enter_context(nc.psum_tensor("flip" + tag, [P, 2 * 512], F32))
        up = ctx.enter_context(nc.psum_tensor("up" + tag, [P, 2, 2 * 512], F32))
        down = ctx.enter_context(nc.psum_tensor("down" + tag, [P, 2 * 512], F32))
        taken, flipped, turned, up_ready, relued, down_ready, biased, y_ready, stored, turn_free = (
            sem(n) for n in ("taken", "flipped", "turned", "up_ready", "relued", "down_ready", "biased", "y_ready",
                             "stored", "turn_free"))
        block = ctx.enter_context(nc.Block())

        @block.sync
        def _(sp):
            sp.sem_inc(turn_free, 1)
            with sp.Fori(0, NTURNS - 1) as it:
                sp.wait_ge(y_ready, it + 1)
                sp.dma_start(out[bass.ds(it * BW, BW), :].rearrange("(b p) f -> p b f", p=P), y[:, :, :]
                             ).then_inc(stored, 16)
                sp.wait_ge(stored, it * 16 + 16)
                sp.sem_inc(turn_free, 1)
            sp.wait_ge(y_ready, NTURNS)
            first = (NTURNS - 1) * BW
            full = (N_NODES - first) // P
            rest = N_NODES - first - full * P
            sp.dma_start(out[first:first + full * P, :].rearrange("(b p) f -> p b f", p=P), y[:, 0:full, :]
                         ).then_inc(stored, 16)
            sp.dma_start(out[first + full * P:N_NODES, :], y[0:rest, full, :]).then_inc(stored, 16)
            sp.wait_ge(stored, 16 * (NTURNS + 1))

        @block.tensor
        def _(pe):
            with pe.Fori(0, NTURNS) as it:
                pe.wait_ge(taken, it + 1)
                for b in range(BG):
                    ins = nc.tensor.transpose(flip[:, b * P:(b + 1) * P], h[:, b, :], env.ident[:, :])
                ins.then_inc(flipped, 1)
                pe.wait_ge(turned, it + 1)
                for c in range(NC):
                    if c >= 2:
                        pe.wait_ge(relued, it * NC + c - 1)
                    for a, b in ((0, 512), (512, BW)):
                        ins = nc.tensor.matmul(up[:, c % 2, a:b], lhsT=env.FW1[:, c * P:(c + 1) * P], rhs=hT[:, a:b],
                                               start=True, stop=True)
                    ins.then_inc(up_ready, 1)
                pe.wait_ge(relued, it * NC + NC)
                for b in range(BG):
                    for c in range(NC):
                        ins = nc.tensor.matmul(down[:, b * P:(b + 1) * P], lhsT=hidden[:, c, b * P:(b + 1) * P],
                                               rhs=env.FW2[:, c, :], start=c == 0, stop=c == NC - 1)
                ins.then_inc(down_ready, 1)

        @block.scalar
        def _(act):
            with act.Fori(0, NTURNS) as it:
                act.wait_ge(flipped, it + 1)
                nc.scalar.copy(hT[:, :], flip[:, 0:BW]).then_inc(turned, 1)
                for c in range(NC):
                    act.wait_ge(up_ready, it * NC + c + 1)
                    nc.scalar.activation(hidden[:, c, :], up[:, c % 2, 0:BW], ACT.Relu, bias=env.fb1[:, c:c + 1]
                                         ).then_inc(relued, 1)

        @block.vector
        def _(dve):
            with dve.Fori(0, NTURNS) as it:
                dve.wait_ge(turn_free, it + 1)
                nc.vector.tensor_copy(h[:, :, :], env.den[:, bass.ds(it * BW, BW)].rearrange(
                    "p (b f) -> p b f", b=BG)).then_inc(taken, 1)
                dve.wait_ge(down_ready, it + 1)
                b2 = env.rows[:, env.row_names.index("L3_gnn_b2"), :].unsqueeze(1).to_broadcast([P, BG, F])
                nc.vector.tensor_tensor(y[:, :, :], down[:, 0:BW].rearrange("p (b f) -> p b f", b=BG), b2, ALU.add
                                        ).then_inc(biased, 1)
                dve.wait_ge(biased, it + 1)
                nc.vector.tensor_tensor(y[:, :, :], y[:, :, :], env.X[:, bass.ds(it * BG, BG), :], ALU.add
                                        ).then_inc(y_ready, 1)


def copy_phase(nc, env, out, in_):
    with ExitStack() as ctx:
        tag = env.tag(ctx)

        loaded = env.semaphore("loaded" + tag)
        block = ctx.enter_context(nc.Block())

        @block.sync
        def _(sp):
            sp.dma_start(out, in_).then_inc(loaded, 16)
            sp.wait_ge(loaded, 16)


def program(nc, ins, out):
    env = Env()
    env.nc = nc
    env.ins = ins
    env.src_groups = ins["src_groups"]
    with ExitStack() as ctx:
        def sb(name, shape, dt=F32):
            return ctx.enter_context(nc.sbuf_tensor(name, shape, dt))

        def dram(name, shape, dt=F32):
            return nc.dram_tensor(name, shape, dt, kind="Internal").ap()

        env.held = ctx.enter_context(nc.semaphore("held"))
        env.X = sb("X", [P, NB, F])
        env.acc = sb("acc", [P, HEADS * NTR])
        env.den = sb("den", [P, HEADS * NTR])
        env.SC = sb("SC", [P, HEADS * NTR])
        env.W = sb("W", [P, NTX * HEADS])
        env.eweight = sb("eweight", [P, NTX])
        env.dloc = sb("dloc", [P, NTX])
        env.starts = sb("starts", [1, NTX], I32)
        env.rowdstf = sb("rowdstf", [P, RB, P])
        env.iota = sb("iota", [P, P])
        env.ident = sb("ident", [P, P])
        env.dis = sb("dis", [P, NB, 2])
        env.logdeg = sb("logdeg", [P, NB])
        env.rden = sb("rden", [P, NB, HEADS])
        env.nmask = sb("nmask", [P, NB, NTYPES])
        env.mu = sb("mu", [P, ETYPES])
        env.L0W1, env.L0W2, env.L2W = sb("L0W1", [P, F]), sb("L0W2", [P, F]), sb("L2W", [P, F])
        env.WQKV = sb("WQKV", [P, NTYPES, 3 * F])
        env.WE = sb("WE", [P, ETYPES, F])
        env.W3 = sb("W3", [P, 2 * FG + F])
        env.FW1, env.FW2, env.fb1 = sb("FW1", [P, FF]), sb("FW2", [P, FF // P, F]), sb("fb1", [P, FF // P])
        env.row_names = ["L0_gnn_b1", "L0_gnn_b2", "L2_gnn_bias", "L3_gnn_ln1_g", "L3_gnn_ln1_b", "L3_gnn_ln2_g",
                         "L3_gnn_ln2_b", "L3_gnn_b2"]
        env.rows = sb("rows_b", [P, len(env.row_names), F])
        env.kidx_groups = dram("kidx_groups", [NG, P, GT], I32)
        env.Htab = dram("Htab", [NPAD, F])
        env.Ktab = dram("Ktab", [NPAD, ETYPES * F])
        env.Qtab = dram("Qtab", [NWIN, F])
        env.Vtab = dram("Vtab", [NPAD, F])
        env.FTtab = dram("FTtab", [NPAD, FG])
        env.Dtab = dram("Dtab", [NWIN, FG])
        env.FEtab = dram("FEtab", [NPAD, F])
        env.Ftab = dram("Ftab", [NPAD, F])
        env.Feat = dram("Feat", [NPAD, F])
        env.edge_scale = env.eweight

        load_phase(nc, env)
        degree_columns_phase(nc, env)
        aggregate_phase(nc, env, None, None, 2, False)
        turn_den_phase(nc, env, 2, "degrees")
        node_phase(nc, env, "start")
        aggregate_phase(nc, env, env.Htab, "edge", 0, False)
        node_phase(nc, env, "conv1")
        aggregate_phase(nc, env, env.Htab, "edge", 0, False)
        node_phase(nc, env, "conv2")
        project_phase(nc, env, "attention")
        keys = env.Ktab.rearrange("n (t f) -> (n t) f", t=ETYPES)
        score_phase(nc, env, keys, env.kidx_groups, env.Qtab, 1, F)
        softmax_phase(nc, env, 1, -1e9, False)
        env.edge_scale = env.W
        aggregate_phase(nc, env, env.Vtab, "edge", 1, True)
        turn_den_phase(nc, env, 1, "attention")
        node_phase(nc, env, "attend")
        aggregate_phase(nc, env, env.Htab, None, 0, False)
        node_phase(nc, env, "conv3")
        project_phase(nc, env, "diffusion")
        score_phase(nc, env, env.FTtab, env.src_groups, env.Dtab, HEADS, FG)
        softmax_phase(nc, env, HEADS, None, True)
        copy_phase(nc, env, env.SC[:, 0:NPAD].rearrange("p (b f) -> p b f", b=NB),
                   env.FEtab.rearrange("(b p) f -> p b f", p=P))
        aggregate_phase(nc, env, env.FEtab, "heads", HEADS, True)
        turn_den_phase(nc, env, HEADS, "diffusion")
        for hop in range(HOPS - 1):
            node_phase(nc, env, "hop")
            aggregate_phase(nc, env, env.Ftab, "heads", 0, True)
        node_phase(nc, env, "last")
        feed_forward_phase(nc, env, out)


def degree_columns_phase(nc, env):
    with ExitStack() as ctx:
        tag = env.tag(ctx)
        done = env.semaphore("done" + tag)
        block = ctx.enter_context(nc.Block())

        @block.vector
        def _(dve):
            w = env.W[:, 0:2 * NT].rearrange("p (t c) -> p t c", c=2)
            nc.vector.memset(w[:, :, 1], 1.0).then_inc(done, 1)
            nc.vector.tensor_copy(w[:, :, 0], env.eweight[:, 0:NT]).then_inc(done, 1)
            dve.wait_ge(done, 2)


def kernel(**inputs):
    import numpy as np
    import concourse.bacc as bacc
    from concourse.bass_utils import run_bass_kernel_spmd as run

    given = {k: np.asarray(v) for k, v in inputs.items()}

    def padded(a, n, value=0):
        return np.concatenate([a, np.full((n - a.shape[0], *a.shape[1:]), value, a.dtype)])

    def grouped(a):
        return np.ascontiguousarray(padded(a, NT * P).reshape(NG, GT, P).transpose(0, 2, 1))

    dst = padded(given["dst"], NTR * P, PAD_NODE)
    by_row = dst.reshape(NTR, P)
    arrays = {
        "x": padded(given["x"], NPAD),
        "src_groups": grouped(given["src"]),
        "etype_groups": grouped(given["edge_type_8"]),
        "eweight": np.ascontiguousarray(padded(given["edge_weight"], NT * P).reshape(NT, P).T),
        "dst_tiles": np.ascontiguousarray(by_row[:NT].T),
        "starts": np.ascontiguousarray(by_row[:NT, 0].reshape(1, NT)),
        "dst_rows": np.ascontiguousarray(by_row.reshape(RB, P, P).transpose(1, 0, 2)),
        "dst_ends": np.ascontiguousarray(by_row[:, [0, P - 1]].T),
        "ntype": np.ascontiguousarray(padded(given["node_type_4"], NPAD).reshape(NB, P).T),
        "L2_WT": np.ascontiguousarray(given["L2_gnn_weight"].T),
        "L3_WhT": np.ascontiguousarray(given["L3_gnn_Wh"].T),
        "L3_WtT": np.ascontiguousarray(given["L3_gnn_Wt"].T),
        "L3_WeT": np.ascontiguousarray(given["L3_gnn_We"].T),
        "L3_W1T": np.ascontiguousarray(given["L3_gnn_W1"].T),
        "L3_W2T": np.ascontiguousarray(given["L3_gnn_W2"].T),
        "L3_b1": np.ascontiguousarray(given["L3_gnn_b1"].reshape(FF // P, P).T),
        "L3_attn": given["L3_gnn_attn_p"].reshape(F),
        "L3_ghead": given["L3_gnn_g_head"].reshape(F),
        "L3_gtail": given["L3_gnn_g_tail"].reshape(F),
    }
    for name in ("L0_gnn_W1", "L0_gnn_W2", "L1_gnn_W_Q", "L1_gnn_W_K", "L1_gnn_W_V", "L1_gnn_W_edge", "L1_gnn_mu",
                 "L0_gnn_b1", "L0_gnn_b2", "L2_gnn_bias", "L3_gnn_ln1_g", "L3_gnn_ln1_b", "L3_gnn_ln2_g",
                 "L3_gnn_ln2_b", "L3_gnn_b2"):
        arrays[name] = np.ascontiguousarray(given[name])

    nc = bacc.Bacc("TRN2", target_bir_lowering=False, num_devices=1)
    ins = {k: nc.dram_tensor(f"in_{k}", v.shape, mybir.dt.from_np(v.dtype), kind="ExternalInput").ap()
           for k, v in arrays.items()}
    out = nc.dram_tensor("out", (N_NODES, F), F32, kind="ExternalOutput").ap()
    program(nc, ins, out)
    result = run(nc, [{f"in_{k}": v for k, v in arrays.items()}], core_ids=[0])
    return result.results[0]["out"]
```

```python
from contextlib import ExitStack

import concourse.bass as bass
from concourse import mybir
from concourse.alu_op_type import AluOpType as ALU

F32, I32, BF16 = mybir.dt.float32, mybir.dt.int32, mybir.dt.bfloat16
ACT = mybir.ActivationFunctionType
AX = mybir.AxisListType

P = 128
N_NODES, N_EDGES = 6250, 106250
F = 128
HEADS, DH = 8, 16
NTYPES, ETYPES = 4, 8
FF = 4 * F
HOPS, ALPHA, EPS = 5, 0.15, 1e-5

NB = -(-N_NODES // P)
NPAD = NB * P
NWIN = NPAD + P
PAD_NODE = N_NODES
GT = 4
RING = 4
TURN = GT * RING
NT = -(-N_EDGES // (P * TURN)) * TURN
NG = NT // GT
TURNS = NT // TURN
BANKS = 4
AHEAD = 2
NTX = NT + AHEAD * GT
RB = -(-NT // P)
NTR = RB * P
BG = 7
NTURNS = NB // BG
BW = BG * P
HALVES = ((0, 4), (4, BG))
FG = F + HEADS
BIG = 1e30
assert NB % BG == 0 and NTR * HEADS >= NWIN


class Env:

    phases = 0

    def tag(self, ctx):
        self.phases += 1
        self.phase_semaphores = []
        ctx.callback(self.clear_semaphores)
        return f"_{self.phases}"

    def semaphore(self, name):
        self.phase_semaphores.append(self.nc.alloc_semaphore(name))
        return self.phase_semaphores[-1]

    def clear_semaphores(self):
        self.nc.clear_and_free_semaphores(self.phase_semaphores)
        self.nc.all_engine_barrier()


def hold(engine, env, semaphore, value):
    engine.wait_ge(semaphore, value)
    engine.sem_inc(env.held, 1)


def onehot_group(nc, env, out, first_tile):
    return nc.vector.tensor_tensor(
        out, env.iota[:, :].unsqueeze(1).to_broadcast([P, GT, P]),
        env.dloc[:, bass.ds(first_tile, GT)].unsqueeze(2).to_broadcast([P, GT, P]), ALU.is_equal)


def window_starts(nc, engine, env, turn, count=1):
    _, starts = nc.values_load_multi_w_load_instructions(
        env.starts[0:1, bass.ds(turn * TURN, count * TURN)], engines=(engine,), min_val=0, max_val=N_NODES,
        skip_runtime_bounds_check_because="a destination is a node's number, and PAD_NODE is N_NODES")
    return starts


def turns(engine, count, body):
    with engine.Fori(0, count - 1) as turn:
        body(turn, False)
    body(count - 1, True)


def load_phase(nc, env):
    with ExitStack() as ctx:
        tag = env.tag(ctx)

        def sb(name, shape, dt=F32):
            return ctx.enter_context(nc.sbuf_tensor(name + tag, shape, dt))

        def sem(name):
            return env.semaphore(name + tag)

        dst_tiles = sb("dst_tiles", [P, NT], I32)
        starts_all = sb("starts_all", [P, NT], I32)
        iota_i = sb("iota_i", [P, P], I32)
        etype = sb("etype", [P, NT], I32)
        src_lin = sb("src_lin", [P, NT], I32)
        kidx = sb("kidx", [P, NT], I32)
        ntype = sb("ntype", [P, NB], I32)
        vecs = sb("vecs", [P, 3, F])
        rowdst = sb("rowdst", [P, RB, P], I32)
        loaded, cleared, ident0, made = sem("loaded"), sem("cleared"), sem("ident0"), sem("made")
        kidx_made, kidx_stored = sem("kidx_made"), sem("kidx_stored")
        vec_done = sem("vec_done")
        zero_stored = sem("zero_stored")
        block = ctx.enter_context(nc.Block())
        I = env.ins
        loads = [
            (dst_tiles[:, :], I["dst_tiles"]),
            (starts_all[:, :], I["starts"].to_broadcast([P, NT])),
            (env.starts[0:1, 0:NT], I["starts"]),
            (src_lin[:, :], I["src_groups"].rearrange("g p u -> (g p u)").rearrange("(a b) -> a b", a=P)),
            (etype[:, :], I["etype_groups"].rearrange("g p u -> (g p u)").rearrange("(a b) -> a b", a=P)),
            (ntype[:, :], I["ntype"]),
            (env.eweight[:, 0:NT], I["eweight"]),
            (env.X[:, :, :], I["x"].rearrange("(b p) f -> p b f", p=P)),
            (rowdst[:, :, :], I["dst_rows"]),
            (env.L0W1[:, :], I["L0_gnn_W1"]), (env.L0W2[:, :], I["L0_gnn_W2"]), (env.L2W[:, :], I["L2_WT"]),
            (env.W3[:, 0:F], I["L3_WhT"]), (env.W3[:, FG:FG + F], I["L3_WtT"]),
            (env.W3[:, 2 * FG:2 * FG + F], I["L3_WeT"]),
        ]
        loads += [(env.rows[:, n, :], I[name].unsqueeze(0).to_broadcast([P, F])) for n, name in enumerate(env.row_names)]
        loads += [(vecs[:, n, :], I[name].unsqueeze(0).to_broadcast([P, F]))
                  for n, name in enumerate(("L3_attn", "L3_ghead", "L3_gtail"))]

        @block.sync
        def _(sp):
            for out, in_ in loads:
                sp.dma_start(out, in_).then_inc(loaded, 16)
            sp.wait_ge(kidx_made, 1)
            sp.dma_start(env.kidx_groups.rearrange("g p u -> (g p u)").rearrange("(a b) -> a b", a=P),
                         kidx[:, :]).then_inc(kidx_stored, 16)
            sp.wait_ge(cleared, 2)
            sp.dma_start(env.Qtab[NPAD:NWIN, :], env.acc[:, 0:F]).then_inc(zero_stored, 16)
            sp.dma_start(env.Dtab[NPAD:NWIN, :], env.acc[:, 0:FG]).then_inc(zero_stored, 16)
            sp.wait_ge(kidx_stored, 16)
            sp.wait_ge(zero_stored, 32)

        @block.gpsimd
        def _(pool):
            pool.memset(env.ident[:, :], 0.0).then_inc(ident0, 1)
            pool.memset(env.SC[:, :], 0.0)
            pool.memset(env.W[:, :], 0.0)
            pool.iota(iota_i[:, :], pattern=[[1, P]], base=0, channel_multiplier=0).then_inc(made, 1)
            pool.wait_ge(ident0, 1)
            pool.affine_select(out=env.ident[:, :], in_=env.ident[:, :], compare_op=ALU.not_equal, fill=1.0,
                               base=0, pattern=[[-1, P]], channel_multiplier=1).then_inc(made, 1)

        @block.vector
        def _(dve):
            V = nc.vector
            done = [0]

            def link(ins):
                done[0] += 1
                ins.then_inc(vec_done, 1)
                dve.wait_ge(vec_done, done[0])

            V.memset(env.dloc[:, :], 0.0).then_inc(cleared, 1)
            V.memset(env.acc[:, :], 0.0).then_inc(cleared, 1)
            link(V.memset(env.eweight[:, NT:NTX], 0.0))
            dve.wait_ge(loaded, 16 * len(loads))
            dve.wait_ge(made, 2)
            V.tensor_copy(env.iota[:, :], iota_i[:, :])
            V.tensor_tensor(env.dloc[:, 0:NT], dst_tiles[:, :], starts_all[:, :], ALU.subtract)
            V.tensor_copy(env.rowdstf[:, :, :], rowdst[:, :, :])
            V.scalar_tensor_tensor(out=kidx[:, :], in0=src_lin[:, :], scalar=float(ETYPES), in1=etype[:, :],
                                   op0=ALU.mult, op1=ALU.add).then_inc(kidx_made, 1)
            for t in range(NTYPES):
                V.tensor_scalar(env.nmask[:, :, t], ntype[:, :], float(t), None, ALU.is_equal)
            tmp = env.acc[:, NWIN - 3 * F:NWIN]
            link(V.tensor_tensor(tmp[:, F:2 * F], env.W3[:, 0:F], vecs[:, 1, :], ALU.mult))
            link(V.tensor_tensor(tmp[:, 2 * F:3 * F], env.W3[:, FG:FG + F], vecs[:, 2, :], ALU.mult))
            V.tensor_reduce(env.W3[:, F:FG], tmp[:, F:2 * F].rearrange("p (h d) -> p h d", h=HEADS), AX.X, ALU.add)
            V.tensor_reduce(env.W3[:, FG + F:2 * FG], tmp[:, 2 * F:3 * F].rearrange("p (h d) -> p h d", h=HEADS),
                            AX.X, ALU.add)
            link(V.tensor_scalar(vecs[:, 0, :], vecs[:, 0, :], 1.0 / DH, None, ALU.mult))
            link(V.tensor_tensor(env.W3[:, FG:FG + F], env.W3[:, FG:FG + F], vecs[:, 0, :], ALU.mult))


def aggregate_phase(nc, env, table, kept, scale, columns, clear, beside=None):
    with ExitStack() as ctx:
        tag = env.tag(ctx)

        def sb(name, shape, dt=F32):
            return ctx.enter_context(nc.sbuf_tensor(name + tag, shape, dt))

        def sem(name):
            return env.semaphore(name + tag)

        M = P if columns is None else columns.shape[2]
        twin = table is None
        pool_slots = (0, 2) if twin else ()
        act_slots = (1,) if twin and scale == "heads" else ()
        assert clear or not twin
        rows = sb("rows", [P, RING, GT, F]) if columns is None else None
        idx = sb("idx", [P, RING, GT], I32) if table is not None else None
        places = sb("places", [P, RING, GT]) if twin else None
        onehot = sb("onehot", [P, RING, GT, P])
        taken = sb("taken", [P, RING, GT, M], BF16) if columns is not None else None
        ready_mark = sb("ready_mark", [P, 1])
        sums = ctx.enter_context(nc.psum_tensor("sums" + tag, [P, BANKS, GT, P], F32))
        idx_loaded = [sem(f"idx_loaded{k}") for k in range(RING)]
        fetched = [sem(f"fetched{k}") for k in range(RING)]
        places_loaded = [sem(f"places_loaded{k}") for k in range(RING)] if twin else None
        built = [sem(f"built{k}") for k in range(RING)]
        scaled, summed, added = (sem(n) for n in ("scaled", "summed", "added"))
        full = 16 * GT if kept is None else 16
        block = ctx.enter_context(nc.Block())

        if twin:
            @block.sync
            def _(sp):
                for k in pool_slots:
                    sp.sem_inc(built[k], 1)
                if beside is not None:
                    beside_loaded = sem("beside_loaded")
                    sp.dma_start(*beside).then_inc(beside_loaded, 16)

                def body(turn, last):
                    for k in range(RING):
                        g = turn * RING + k
                        if k in pool_slots:
                            sp.wait_ge(built[k], turn + 1)
                            sp.dma_start(places[:, k, :], env.dloc[:, bass.ds(g * GT, GT)]
                                         ).then_inc(places_loaded[k], 16)
                        if kept is None:
                            continue
                        sp.wait_ge(summed, g + 1)
                        sp.dma_start(rows[:, k, :, :].rearrange("p u f -> p (u f)"),
                                     kept[bass.ds(g, 1), :, :].rearrange("a p f -> (a p) f")
                                     ).then_inc(fetched[k], 16)
                turns(sp, TURNS, body)
                if beside is not None:
                    sp.wait_ge(beside_loaded, 16)

        if table is not None:
            @block.sync
            def _(sp):
                def body(turn, last):
                    for k in range(RING):
                        g = turn * RING + k
                        sp.wait_ge(summed, g + 1)
                        sp.dma_start(idx[:, k, :], env.src_groups[bass.ds(g, 1), :, :].rearrange("a p u -> (a p) u")
                                     ).then_inc(idx_loaded[k], 16)
                turns(sp, TURNS, body)

            @block.gpsimd
            def _(pool):
                def body(turn, last):
                    for k in range(RING):
                        pool.wait_ge(summed, turn * RING + k + 1)
                        hold(pool, env, idx_loaded[k], turn * 16 + 16)
                        for u in range(GT):
                            nc.gpsimd.indirect_dma_start(
                                rows[:, k, u, :], None, table,
                                bass.IndirectOffsetOnAxis(ap=idx[:, k, u:u + 1], axis=0)).then_inc(fetched[k], 16)
                turns(pool, TURNS, body)

        if columns is not None or scale == "edge":
            @block.scalar
            def _(act):
                def body(turn, last):
                    for k in range(RING):
                        g = turn * RING + k
                        t = g * GT
                        if columns is not None:
                            hold(act, env, summed, g + 1)
                            nc.scalar.copy(taken[:, k, :, :], columns[:, bass.ds(t, GT), :]).then_inc(scaled, 1)
                        else:
                            hold(act, env, fetched[k], turn * full + full)
                            for u in range(GT):
                                ins = nc.scalar.activation(rows[:, k, u, :], rows[:, k, u, :], ACT.Copy,
                                                           scale=env.edge_scale[:, bass.ds(t + u, 1)])
                            ins.then_inc(scaled, 1)
                turns(act, TURNS, body)

        if twin:
            @block.gpsimd
            def _(pool):
                def body(turn, last):
                    for k in pool_slots:
                        g = turn * RING + k
                        pool.wait_ge(summed, g + 1)
                        hold(pool, env, places_loaded[k], turn * 16 + 16)
                        for u in range(GT):
                            ins = nc.gpsimd.tensor_scalar(onehot[:, k, u, :], env.iota[:, :], places[:, k, u:u + 1],
                                                          None, ALU.is_equal)
                        ins.then_inc(built[k], 1)
                turns(pool, TURNS, body)

        if act_slots:
            distances_ready = sem("distances_ready")

            @block.scalar
            def _(act):
                def body(turn, last):
                    for k in act_slots:
                        g = turn * RING + k
                        slot = onehot[:, k, :, :]
                        hold(act, env, summed, g + 1)
                        for u in range(GT):
                            ins = nc.scalar.activation(onehot[:, k, u, :], env.iota[:, :], ACT.Abs,
                                                       bias=env.dloc[:, bass.ds(g * GT + u, 1)], scale=-1.0)
                        ins.then_inc(distances_ready, 1)
                        act.wait_ge(distances_ready, turn * len(act_slots) + act_slots.index(k) + 1)
                        nc.scalar.activation(slot, slot, ACT.Relu, bias=1.0, scale=-1.0).then_inc(built[k], 1)
                turns(act, TURNS, body)

        @block.tensor
        def _(pe):
            pe.sem_inc(summed, RING)

            def body(turn, last):
                for k in range(RING):
                    g = turn * RING + k
                    pe.wait_ge(built[k], turn + (2 if k in pool_slots else 1))
                    pe.wait_ge(added, g * GT + GT)
                    if columns is None and scale is None:
                        pe.wait_ge(fetched[k], turn * full + full)
                    else:
                        pe.wait_ge(scaled, g + 1)
                    for u in range(GT):
                        if columns is not None:
                            upper = onehot[:, k, u, :].bitcast(BF16)[:, 1::2]
                            ins = nc.tensor.matmul(sums[0:M, k % BANKS, u, :], lhsT=taken[:, k, u, :], rhs=upper,
                                                   start=True, stop=True)
                        else:
                            ins = nc.tensor.matmul(sums[:, k % BANKS, u, :], lhsT=rows[:, k, u, :],
                                                   rhs=onehot[:, k, u, :], start=True, stop=True)
                    ins.then_inc(summed, 1)
            turns(pe, TURNS, body)

        @block.vector
        def _(dve):
            def build(g, k):
                onehot_group(nc, env, onehot[:, k, :, :], g * GT).then_inc(built[k], 1)

            def scale_rows(turn, k):
                g = turn * RING + k
                dve.wait_ge(fetched[k], turn * full + full)
                v = rows[:, k, :, :].rearrange("p u (h d) -> p (u h) d", d=DH)
                w = env.W[:, bass.ds(g * GT * HEADS, GT * HEADS)].unsqueeze(2).to_broadcast([P, GT * HEADS, DH])
                nc.vector.tensor_tensor(v, v, w, ALU.mult).then_inc(scaled, 1)

            for g in range(RING if twin else AHEAD):
                if g not in pool_slots + act_slots:
                    build(g, g)
            if clear:
                nc.vector.memset(env.acc[0:M, 0:NWIN], 0.0)
            if twin:
                nc.vector.memset(env.den[0:M, 0:NWIN], 0.0)
            nc.vector.memset(ready_mark[:, :], 0.0).then_inc(added, BANKS * GT)
            lead = 2 if twin else 1
            if scale == "heads":
                for k in range(lead):
                    scale_rows(0, k)

            def add_turn(turn, last, starts):
                for k in range(RING):
                    g = turn * RING + k
                    if scale == "heads" and not (last and k >= RING - lead):
                        scale_rows(turn + (k + lead) // RING, (k + lead) % RING)
                    dve.wait_ge(summed, g + RING + 1)
                    for u in range(GT):
                        dve.wait_ge(added, g * GT + u + BANKS * GT - (1 if twin else 0))
                        total = env.den if twin and u % 2 else env.acc
                        a = total[0:M, bass.ds(starts[k * GT + u], P)]
                        nc.vector.tensor_tensor(a, a, sums[0:M, k % BANKS, u, :], ALU.add).then_inc(added, 1)
                    if twin and k not in pool_slots + act_slots and not last:
                        build(g + RING, k)
                    if not twin and not (last and k >= RING - AHEAD):
                        build(g + AHEAD, (k + AHEAD) % RING)
            together = 2 if twin and TURNS % 2 == 0 else 1

            def body(step, last):
                starts = window_starts(nc, mybir.EngineType.DVE, env, step * together, together)
                for n in range(together):
                    add_turn(step * together + n, last and n == together - 1, starts[n * TURN:(n + 1) * TURN])
            turns(dve, TURNS // together, body)
            if twin:
                dve.wait_ge(added, NT + BANKS * GT)
                a = env.acc[0:M, 0:NWIN]
                nc.vector.tensor_tensor(a, a, env.den[0:M, 0:NWIN], ALU.add)


def score_phase(nc, env, table, index_groups, windows, kept, heads, width):
    with ExitStack() as ctx:
        tag = env.tag(ctx)

        def sb(name, shape, dt=F32):
            return ctx.enter_context(nc.sbuf_tensor(name + tag, shape, dt))

        def sem(name):
            return env.semaphore(name + tag)

        rows = sb("rows", [P, RING, GT, width + F])
        idx = sb("idx", [P, RING, GT], I32)
        onehot = sb("onehot", [P, RING, GT, P])
        win = sb("win", [P, RING, GT, width])
        spread = sb("spread", [P, 2, GT, P])
        flip = ctx.enter_context(nc.psum_tensor("flip" + tag, [P, 2, GT, P], F32))
        want = ctx.enter_context(nc.psum_tensor("want" + tag, [P, 2, GT, 2 * P], F32))
        idx_loaded = [sem(f"idx_loaded{k}") for k in range(RING)]
        gathered = [sem(f"gathered{k}") for k in range(RING)]
        win_loaded = [sem(f"win_loaded{k}") for k in range(RING)]
        kept_stored = [sem(f"kept_stored{k}") for k in range(RING)]
        built, flipped, spread_ready, wanted, multiplied, scored = (sem(n) for n in (
            "built", "flipped", "spread_ready", "wanted", "multiplied", "scored"))
        block = ctx.enter_context(nc.Block())

        @block.sync
        def _(sp):
            def body(turn, last):
                starts = window_starts(nc, mybir.EngineType.SP, env, turn)
                for k in range(RING):
                    g = turn * RING + k
                    sp.wait_ge(scored, g + 1)
                    sp.dma_start(idx[:, k, :], index_groups[bass.ds(g, 1), :, :].rearrange("a p u -> (a p) u")
                                 ).then_inc(idx_loaded[k], 16)
                    for u in range(GT):
                        sp.dma_start(win[:, k, u, :], windows[bass.ds(starts[k * GT + u], P), :]
                                     ).then_inc(win_loaded[k], 16)
            turns(sp, TURNS, body)

        @block.gpsimd
        def _(pool):
            def body(turn, last):
                for k in range(RING):
                    hold(pool, env, kept_stored[k], turn * 16 + 16)
                    pool.wait_ge(scored, turn * RING + k + 1)
                    hold(pool, env, idx_loaded[k], turn * 16 + 16)
                    for u in range(GT):
                        nc.gpsimd.indirect_dma_start(
                            rows[:, k, u, :], None, table,
                            bass.IndirectOffsetOnAxis(ap=idx[:, k, u:u + 1], axis=0)).then_inc(gathered[k], 16)
            turns(pool, TURNS, body)

        @block.tensor
        def _(pe):
            def body(turn, last):
                for k in range(RING):
                    g = turn * RING + k
                    pe.wait_ge(built, g + 1)
                    pe.wait_ge(scored, g + RING - 1)
                    for u in range(GT):
                        ins = nc.tensor.transpose(flip[:, k % 2, u, :], onehot[:, k, u, :], env.ident[:, :])
                    ins.then_inc(flipped, 1)
                    pe.wait_ge(spread_ready, g + 1)
                    pe.wait_ge(win_loaded[k], turn * 16 * GT + 16 * GT)
                    for u in range(GT):
                        ins = nc.tensor.matmul(want[:, k % 2, u, 0:width], lhsT=spread[:, k % 2, u, :],
                                               rhs=win[:, k, u, :], start=True, stop=True)
                    ins.then_inc(wanted, 1)
            turns(pe, TURNS, body)

        @block.scalar
        def _(act):
            for k in range(RING):
                act.sem_inc(kept_stored[k], 16)

            def body(turn, last):
                for k in range(RING):
                    g = turn * RING + k
                    act.wait_ge(scored, g + RING - 1)
                    act.wait_ge(flipped, g + 1)
                    nc.scalar.copy(spread[:, k % 2, :, :], flip[:, k % 2, :, :]).then_inc(spread_ready, 1)
                    act.wait_ge(gathered[k], turn * 16 * GT + 16 * GT)
                    act.dma_start(kept[bass.ds(g, 1), :, :].rearrange("a p (u f) -> (a p) u f", u=GT),
                                  rows[:, k, :, width:width + F]).then_inc(kept_stored[k], 16)
            turns(act, TURNS, body)
            for k in range(RING):
                act.wait_ge(kept_stored[k], 16 * TURNS + 16)

        @block.vector
        def _(dve):
            def build(g, k):
                onehot_group(nc, env, onehot[:, k, :, :], g * GT).then_inc(built, 1)

            for g in range(AHEAD):
                build(g, g)
            dve.sem_inc(scored, RING)
            score_h = env.SC[:, 0:heads * NTR].rearrange("p (h t) -> p t h", h=heads)
            gate_h = env.W[:, 0:HEADS * NTR].rearrange("p (h t) -> p t h", h=HEADS)

            def body(turn, last):
                for k in range(RING):
                    g = turn * RING + k
                    t = g * GT
                    dve.wait_ge(wanted, g + 1)
                    dve.wait_ge(gathered[k], turn * 16 * GT + 16 * GT)
                    head_rows = rows[:, k, :, 0:F]
                    nc.vector.tensor_tensor(head_rows, head_rows, want[:, k % 2, :, 0:F], ALU.mult
                                            ).then_inc(multiplied, 1)
                    if width > F:
                        nc.vector.tensor_tensor(gate_h[:, bass.ds(t, GT), :], rows[:, k, :, F:width],
                                                want[:, k % 2, :, F:width], ALU.add)
                    if not (last and k >= RING - AHEAD):
                        build(g + AHEAD, (k + AHEAD) % RING)
                    dve.wait_ge(multiplied, g + 1)
                    nc.vector.tensor_reduce(
                        score_h[:, bass.ds(t, GT), :], head_rows.rearrange("p u (h d) -> p u h d", h=heads), AX.X,
                        ALU.add).then_inc(scored, 1)
            turns(dve, TURNS, body)


def softmax_phase(nc, env, heads, floor, tiny, factor, gated):
    with ExitStack() as ctx:
        tag = env.tag(ctx)

        def sb(name, shape, dt=F32):
            return ctx.enter_context(nc.sbuf_tensor(name + tag, shape, dt))

        def sem(name):
            return env.semaphore(name + tag)

        ends = sb("ends", [heads, 2, NTR])
        ends_dst = sb("ends_dst", [heads, 2, NTR], I32)
        carried = ends_dst[:, :, :].bitcast(F32)
        cont = sb("cont", [heads, NTR + 1])
        passes = sb("passes", [heads, 2, NTR])
        same = sb("same", [P, NTR + 1])
        carry = sb("carry", [P, 2, heads, RB])
        edge_of = sb("edge_of", [P, RB, P])
        square = ctx.enter_context(nc.psum_tensor("square" + tag, [P, 2, 2 * 512], F32))
        turned = ctx.enter_context(nc.psum_tensor("turned" + tag, [P, 2, 2 * 512], F32))
        (ends_loaded, rowed, row_copied, scanned, end_turned, chain, carry_ready, carry_turned, shifted, exped,
         gate_rowed, gate_copied, weighted, unrowed, un_copied) = (sem(n) for n in (
             "ends_loaded", "rowed", "row_copied", "scanned", "end_turned", "chain", "carry_ready", "carry_turned",
             "shifted", "exped", "gate_rowed", "gate_copied", "weighted", "unrowed", "un_copied"))
        block = ctx.enter_context(nc.Block())
        n_all = heads * NTR
        S_rows, M_rows, T_rows = (buf[:, 0:n_all].rearrange("p (h b e) -> p h b e", h=heads, b=RB)
                                  for buf in (env.acc, env.den, env.SC))

        def head(buf, h):
            return buf[:, h * NTR:(h + 1) * NTR]

        @block.sync
        def _(sp):
            sp.dma_start(ends_dst[:, :, :], env.ins["dst_ends"].unsqueeze(0).to_broadcast([heads, 2, NTR])
                         ).then_inc(ends_loaded, 16)
            sp.wait_ge(ends_loaded, 16)

        @block.tensor
        def _(pe):
            def turn_head(buf, h, signal):
                for b in range(RB):
                    ins = nc.tensor.transpose(square[:, h % 2, b * P:(b + 1) * P],
                                              buf[:, h * NTR + b * P:h * NTR + (b + 1) * P], env.ident[:, :])
                ins.then_inc(signal, 1)

            def turn_ends(round_):
                pe.wait_ge(scanned, round_ + 1)
                for side, at in ((0, 0), (1, P - 1)):
                    for b in range(RB):
                        ins = nc.tensor.transpose(turned[0:heads, side, b * P:(b + 1) * P], M_rows[:, :, b, at],
                                                  env.ident[:, :])
                ins.then_inc(end_turned, 1)
                pe.wait_ge(carry_ready, round_ + 1)
                for side in range(2):
                    for b in range(RB):
                        ins = nc.tensor.transpose(turned[:, side, b * heads:(b + 1) * heads],
                                                  carried[:, side, b * P:(b + 1) * P], env.ident[0:heads, 0:heads])
                ins.then_inc(carry_turned, 1)

            for h in range(heads):
                if h >= 2:
                    pe.wait_ge(row_copied, h - 1)
                turn_head(env.SC, h, rowed)
            turn_ends(0)
            pe.wait_ge(row_copied, heads)
            if gated:
                for h in range(heads):
                    if h >= 2:
                        pe.wait_ge(gate_copied, h - 1)
                    turn_head(env.W, h, gate_rowed)
                pe.wait_ge(gate_copied, heads)
            turn_ends(1)
            for h in range(heads):
                if h >= 2:
                    pe.wait_ge(un_copied, h - 1)
                pe.wait_ge(weighted, h + 1)
                turn_head(env.acc, h, unrowed)

        @block.scalar
        def _(act):
            for h in range(heads):
                act.wait_ge(rowed, h + 1)
                nc.scalar.copy(head(env.acc, h), square[:, h % 2, 0:NTR]).then_inc(row_copied, 1)
            act.wait_ge(shifted, 1)
            nc.scalar.activation(env.acc[:, 0:n_all], env.acc[:, 0:n_all], ACT.Exp).then_inc(exped, 1)
            if gated:
                for h in range(heads):
                    act.wait_ge(gate_rowed, h + 1)
                    nc.scalar.activation(head(env.den, h), square[:, h % 2, 0:NTR], ACT.Sigmoid
                                         ).then_inc(gate_copied, 1)
            w = env.W[:, 0:NT * heads].rearrange("p (t h) -> p t h", h=heads)
            for h in range(heads):
                act.wait_ge(unrowed, h + 1)
                nc.scalar.mul(w[:, :, h], square[:, h % 2, 0:NT], factor).then_inc(un_copied, 1)

        @block.vector
        def _(dve):
            V = nc.vector
            done = [0]

            def link(ins):
                done[0] += 1
                ins.then_inc(chain, 1)
                dve.wait_ge(chain, done[0])

            def carry_across(round_, op_pass, op_join, neutral, flags):
                dve.wait_ge(end_turned, round_ + 1)
                link(V.tensor_copy(ends[:, :, :], turned[0:heads, :, 0:NTR]))
                V.tensor_tensor_scan(ends[:, 1, :], passes[:, 0, :], ends[:, 1, :], neutral, op_pass, op_join)
                back = ends[:, 0, :][:, ::-1]
                link(V.tensor_tensor_scan(back, passes[:, 1, :][:, ::-1], back, neutral, op_pass, op_join))
                V.memset(carried[:, 0, 0:1], neutral)
                V.memset(carried[:, 1, NTR - 1:NTR], neutral)
                V.tensor_tensor(carried[:, 0, 1:NTR], ends[:, 1, 0:NTR - 1], cont[:, 1:NTR], op_pass)
                V.tensor_tensor(carried[:, 1, 0:NTR - 1], ends[:, 0, 1:NTR], cont[:, 1:NTR], op_pass
                                ).then_inc(carry_ready, 1)
                dve.wait_ge(carry_turned, round_ + 1)
                for side in range(2):
                    ins = V.tensor_copy(carry[:, side, :, :], turned[:, side, 0:RB * heads].rearrange(
                        "p (b h) -> p h b", b=RB))
                link(ins)
                for side in range(2):
                    end = env.rowdstf[:, :, side * (P - 1):side * (P - 1) + 1].to_broadcast([P, RB, P])
                    link(V.tensor_tensor(edge_of[:, :, :], env.rowdstf[:, :, :], end, ALU.is_equal))
                    if flags:
                        link(V.tensor_scalar(edge_of[:, :, :], edge_of[:, :, :], -1.0, BIG, ALU.add, ALU.mult))
                    for h in range(heads):
                        c = carry[:, side, h, :].unsqueeze(2).to_broadcast([P, RB, P])
                        ins = V.tensor_tensor(T_rows[:, h, :, :], c, edge_of[:, :, :], op_pass)
                    link(ins)
                    link(V.tensor_tensor(M_rows, M_rows, T_rows, op_join))

            dve.wait_ge(ends_loaded, 16)
            V.memset(cont[:, :], 0.0)
            V.memset(same[:, :], 0.0)
            link(V.tensor_copy(ends[:, :, :], ends_dst[:, :, :]))
            flag = same[:, 0:NTR].rearrange("p (b e) -> p b e", b=RB)
            V.tensor_tensor(flag[:, :, 1:P], env.rowdstf[:, :, 1:P], env.rowdstf[:, :, 0:P - 1], ALU.is_equal)
            V.tensor_tensor(cont[:, 1:NTR], ends[:, 0, 1:NTR], ends[:, 1, 0:NTR - 1], ALU.is_equal)
            link(V.tensor_tensor(passes[:, 1, :], ends[:, 0, :], ends[:, 1, :], ALU.is_equal))
            link(V.tensor_tensor(passes[:, 0, :], passes[:, 1, :], cont[:, 0:NTR], ALU.mult))
            link(V.tensor_tensor(passes[:, 1, :], passes[:, 1, :], cont[:, 1:NTR + 1], ALU.mult))
            for flags in (same[:, :], cont[:, :], passes[:, :, :]):
                ins = V.tensor_scalar(flags, flags, -1.0, BIG, ALU.add, ALU.mult)
            link(ins)
            for h in range(heads):
                dve.wait_ge(row_copied, h + 1)
                ins = V.tensor_tensor_scan(head(env.den, h), same[:, 0:NTR], head(env.acc, h), -BIG, ALU.add, ALU.max)
            link(ins)
            for h in range(heads):
                m = head(env.den, h)[:, ::-1]
                ins = V.tensor_tensor_scan(m, same[:, 1:NTR + 1][:, ::-1], m, -BIG, ALU.add, ALU.max)
            ins.then_inc(scanned, 1)
            carry_across(0, ALU.add, ALU.max, -BIG, True)
            if floor is not None:
                link(V.tensor_scalar(M_rows, M_rows, floor, None, ALU.max))
            V.tensor_tensor(S_rows, S_rows, M_rows, ALU.subtract).then_inc(shifted, 1)
            for flags in (same[:, :], cont[:, :], passes[:, :, :]):
                ins = V.tensor_scalar(flags, flags, 0.0, None, ALU.is_equal)
            link(ins)
            dve.wait_ge(exped, 1)
            if gated:
                dve.wait_ge(gate_copied, heads)
                link(V.tensor_tensor(S_rows, S_rows, M_rows, ALU.mult))
            for h in range(heads):
                ins = V.tensor_tensor_scan(head(env.den, h), same[:, 0:NTR], head(env.acc, h), 0.0, ALU.mult, ALU.add)
            link(ins)
            for h in range(heads):
                m = head(env.den, h)[:, ::-1]
                ins = V.tensor_tensor_scan(m, same[:, 1:NTR + 1][:, ::-1], m, 0.0, ALU.mult, ALU.max)
            ins.then_inc(scanned, 1)
            carry_across(1, ALU.mult, ALU.add, 0.0, False)
            if tiny:
                link(V.tensor_scalar(M_rows, M_rows, tiny, None, ALU.add))
            link(V.reciprocal(M_rows, M_rows))
            for h in range(heads):
                V.tensor_tensor(head(env.acc, h), head(env.acc, h), head(env.den, h), ALU.mult
                                ).then_inc(weighted, 1)


PARTS = 3
NCOLS = PARTS + 1


def degrees_phases(nc, env):
    with ExitStack() as outer:
        columns = outer.enter_context(nc.sbuf_tensor("columns", [P, NT, NCOLS], BF16))
        rest = outer.enter_context(nc.sbuf_tensor("rest", [P, NT], F32))
        with ExitStack() as ctx:
            tag = env.tag(ctx)
            chain = env.semaphore("chain" + tag)
            block = ctx.enter_context(nc.Block())

            @block.vector
            def _(dve):
                V = nc.vector
                done = [0]

                def link(ins):
                    done[0] += 1
                    ins.then_inc(chain, 1)
                    dve.wait_ge(chain, done[0])

                V.memset(columns[:, :, PARTS], 1.0)
                left = env.eweight[:, 0:NT]
                for part in range(PARTS):
                    link(V.tensor_copy(columns[:, :, part], left))
                    link(V.tensor_tensor(rest[:, :], left, columns[:, :, part], ALU.subtract))
                    left = rest[:, :]
        aggregate_phase(nc, env, None, None, None, columns, True)
    with ExitStack() as ctx:
        tag = env.tag(ctx)
        nodes = ctx.enter_context(nc.sbuf_tensor("nodes" + tag, [P, NB, NCOLS], F32))
        degree = ctx.enter_context(nc.sbuf_tensor("degree" + tag, [P, NB, 2], F32))
        turned = ctx.enter_context(nc.psum_tensor("turned" + tag, [P, 512], F32))
        sums_turned, chain, to_root, rooted = (env.semaphore(n + tag) for n in (
            "sums_turned", "chain", "to_root", "rooted"))
        block = ctx.enter_context(nc.Block())

        @block.tensor
        def _(pe):
            for b in range(NB):
                ins = nc.tensor.transpose(turned[:, b * NCOLS:(b + 1) * NCOLS], env.acc[0:NCOLS, b * P:(b + 1) * P],
                                          env.ident[0:NCOLS, 0:NCOLS])
            ins.then_inc(sums_turned, 1)

        @block.scalar
        def _(act):
            act.wait_ge(to_root, 1)
            nc.scalar.activation(env.dis[:, :, :], env.dis[:, :, :], ACT.Sqrt)
            nc.scalar.activation(env.logdeg[:, :], env.logdeg[:, :], ACT.Ln).then_inc(rooted, 1)

        @block.vector
        def _(dve):
            V = nc.vector
            done = [0]

            def link(ins):
                done[0] += 1
                ins.then_inc(chain, 1)
                dve.wait_ge(chain, done[0])

            dve.wait_ge(sums_turned, 1)
            link(V.tensor_copy(nodes[:, :, :], turned[:, 0:NB * NCOLS].rearrange("p (b h) -> p b h", b=NB)))
            link(V.tensor_tensor(degree[:, :, 0], nodes[:, :, 0], nodes[:, :, 1], ALU.add))
            link(V.tensor_tensor(degree[:, :, 0], degree[:, :, 0], nodes[:, :, 2], ALU.add))
            V.tensor_copy(degree[:, :, 1], nodes[:, :, PARTS])
            link(V.tensor_scalar(env.logdeg[:, :], nodes[:, :, PARTS], 1.0, None, ALU.max))
            link(V.tensor_scalar(degree[:, :, :], degree[:, :, :], 1.0, None, ALU.add))
            V.tensor_scalar(env.dis[:, :, :], degree[:, :, :], 1e-30, None, ALU.max).then_inc(to_root, 1)
            dve.wait_ge(rooted, 1)
            V.tensor_scalar(degree[:, :, :], degree[:, :, :], 0.0, None, ALU.is_gt)
            link(V.reciprocal(env.dis[:, :, :], env.dis[:, :, :]))
            link(V.tensor_tensor(env.dis[:, :, :], env.dis[:, :, :], degree[:, :, :], ALU.mult))


class Norm:

    def __init__(self, nc, env, ctx, tag):
        self.nc = nc
        self.stats = ctx.enter_context(nc.sbuf_tensor(f"stats{tag}", [P, BG, 6], F32))
        self.mv = ctx.enter_context(nc.sbuf_tensor(f"mv{tag}", [P, BG, 2], F32))
        self.root = ctx.enter_context(nc.sbuf_tensor(f"root{tag}", [P, BG], F32))
        self.rstd = ctx.enter_context(nc.sbuf_tensor(f"rstd{tag}", [P, BG], F32))
        self.shift = ctx.enter_context(nc.sbuf_tensor(f"shift{tag}", [P, BG], F32))
        self.moments, self.rooted, self.factors = (
            [env.semaphore(f"{name}{half}{tag}") for half in range(len(HALVES))]
            for name in ("moments", "rooted", "factors"))

    def take_moments(self, half, src, link):
        V = self.nc.vector
        a, z = HALVES[half]
        for b in range(a, z):
            ins = V.bn_stats(self.stats[:, b, :], src(b))
        link(ins)
        for b in range(a, z):
            ins = V.bn_aggr(self.mv[:, b, :], self.stats[:, b, :])
        link(ins)
        V.tensor_scalar(self.root[:, a:z], self.mv[:, a:z, 1], EPS, None, ALU.add).then_inc(self.moments[half], 1)

    def make_factors(self, dve, it, half, link):
        V = self.nc.vector
        a, z = HALVES[half]
        dve.wait_ge(self.rooted[half], it + 1)
        link(V.reciprocal(self.rstd[:, a:z], self.root[:, a:z]))
        V.scalar_tensor_tensor(out=self.shift[:, a:z], in0=self.mv[:, a:z, 0], scalar=-1.0, in1=self.rstd[:, a:z],
                               op0=ALU.mult, op1=ALU.mult).then_inc(self.factors[half], 1)

    def take_root(self, act, it, half):
        a, z = HALVES[half]
        act.wait_ge(self.moments[half], it + 1)
        self.nc.scalar.activation(self.root[:, a:z], self.root[:, a:z], ACT.Sqrt).then_inc(self.rooted[half], 1)

    def apply(self, half, src, out, func):
        for b in range(*HALVES[half]):
            ins = self.nc.scalar.activation(out(b), src(b), func, bias=self.shift[:, b:b + 1],
                                            scale=self.rstd[:, b:b + 1])
        return ins


class Links:

    def __init__(self, dve, env, sem, it, steps, before=0):
        self.env = env
        self.dve, self.sem, self.steps, self.it, self.n = dve, sem, steps, it, before
        self.before = before

    def __call__(self, ins):
        self.n += 1
        ins.then_inc(self.sem, 1)
        hold(self.dve, self.env, self.sem, self.it * self.steps + self.n)

    def close(self):
        assert self.n - self.before == self.steps, self.n


def node_phase(nc, env, kind):
    with ExitStack() as ctx:
        tag = env.tag(ctx)

        def sb(name, shape, dt=F32):
            return ctx.enter_context(nc.sbuf_tensor(name + tag, shape, dt))

        def sem(name):
            return env.semaphore(name + tag)

        def sems(name):
            return [sem(f"{name}{half}") for half in both]

        both = range(len(HALVES))
        take = kind != "start"
        weight = {"conv1": env.L0W1, "conv2": env.L0W2, "conv3": env.L2W}.get(kind)
        bias = {"conv1": 0, "conv2": 1, "conv3": 2}.get(kind)
        factor = {"start": 0, "conv1": 0, "conv2": 0, "attend": 1, "conv3": 1}.get(kind)
        normed = kind not in ("conv1", "hop")
        refill = kind in ("start", "conv1", "attend")
        staged = sb("staged", [P, BW])
        y = sb("y", [P, BG, F])
        h = sb("h", [P, BG, F])
        outrow = sb("outrow", [P, BG, F])
        feat = sb("feat", [P, BG, F]) if kind == "last" else None
        norm = Norm(nc, env, ctx, "_a" + tag)
        norm2 = Norm(nc, env, ctx, "_b" + tag)
        prod = ctx.enter_context(nc.psum_tensor("prod" + tag, [P, 2 * 512], F32))
        flip = ctx.enter_context(nc.psum_tensor("flip" + tag, [P, 2 * 512], F32))
        chain = sem("chain")
        acc_staged, y_ready, h_ready, feat_loaded = (sems(n) for n in ("acc_staged", "y_ready", "h_ready",
                                                                       "feat_loaded"))
        (product_ready, product_taken, rows_ready, stored, flipped, refilled, feat_taken) = (sems(n) for n in (
            "product_ready", "product_taken", "rows_ready", "stored", "flipped", "refilled", "feat_taken"))
        product_free = rows_ready if kind == "hop" else product_taken
        block = ctx.enter_context(nc.Block())
        table = {"start": env.Htab, "conv1": env.Htab, "attend": env.Htab, "hop": env.Ftab, "conv3": env.Feat}.get(kind)
        stored_rows = h if kind == "conv3" else outrow

        def cols(half):
            a, z = HALVES[half]
            return a * P, z * P

        def table_rows(tab, it, half):
            a, z = HALVES[half]
            return tab[bass.ds(it * BW + a * P, (z - a) * P), :].rearrange("(b p) f -> p b f", p=P)

        def x_block(it, b):
            return env.X[:, bass.ds(it * BG + b, 1), :].rearrange("p a f -> p (a f)")

        def den_block(it, b):
            return env.den[:, bass.ds(it * BW + b * P, P)]

        def before(it):
            return it + 1

        def now(it):
            return it + 2

        @block.sync
        def _(sp):
            for half in both:
                sp.sem_inc(stored[half], 16)
            with sp.Fori(0, NTURNS) as it:
                if kind == "last":
                    for half in both:
                        a, z = HALVES[half]
                        sp.wait_ge(feat_taken[half], before(it))
                        sp.dma_start(feat[:, a:z, :], table_rows(env.Feat, it, half)).then_inc(feat_loaded[half], 16)
                if table is not None:
                    for half in both:
                        a, z = HALVES[half]
                        sp.wait_ge(rows_ready[half], now(it))
                        sp.dma_start(table_rows(table, it, half), stored_rows[:, a:z, :]).then_inc(stored[half], 16)
            if table is not None:
                for half in both:
                    sp.wait_ge(stored[half], 16 * NTURNS + 16)

        def stage(engine, copy, it, half):
            a, z = cols(half)
            hold(engine, env, product_ready[half], before(it))
            copy(staged[:, a:z], env.acc[:, bass.ds(it * BW + a, z - a)]).then_inc(acc_staged[half], 1)

        act_stages = (0,) if kind == "hop" else ()

        if take:
            @block.gpsimd
            def _(pool):
                with pool.Fori(0, NTURNS) as it:
                    for half in both:
                        if half not in act_stages:
                            stage(pool, nc.gpsimd.tensor_copy, it, half)

        if take or refill:
            @block.tensor
            def _(pe):
                def multiply(it):
                    for half in both:
                        pe.wait_ge(acc_staged[half], it + 1)
                        pe.wait_ge(product_free[half], before(it))
                        for b in range(*HALVES[half]):
                            part = staged[:, b * P:(b + 1) * P]
                            if weight is not None:
                                ins = nc.tensor.matmul(prod[:, b * P:(b + 1) * P], lhsT=part, rhs=weight[:, :],
                                                       start=True, stop=True)
                            else:
                                ins = nc.tensor.transpose(prod[:, b * P:(b + 1) * P], part, env.ident[:, :])
                        ins.then_inc(product_ready[half], 1)

                def turn_back(it):
                    for half in both:
                        pe.wait_ge(refilled[half], before(it))
                        pe.wait_ge(rows_ready[half], now(it))
                        for b in range(*HALVES[half]):
                            ins = nc.tensor.transpose(flip[:, b * P:(b + 1) * P], outrow[:, b, :], env.ident[:, :])
                        ins.then_inc(flipped[half], 1)

                for half in both:
                    pe.sem_inc(product_ready[half], 1)
                    pe.sem_inc(flipped[half], 1)
                if take:
                    multiply(0)
                with pe.Fori(0, NTURNS - 1) as it:
                    if take:
                        multiply(it + 1)
                    if refill:
                        turn_back(it)
                if refill:
                    turn_back(NTURNS - 1)

        skewed = normed

        @block.scalar
        def _(act):
            for half in both:
                act.sem_inc(refilled[half], 1)
            if skewed:
                for half in both:
                    norm.take_root(act, 0, half)

            def body(it, last):
                for half in act_stages:
                    stage(act, nc.scalar.copy, it, half)
                if normed and not skewed:
                    for half in both:
                        norm.take_root(act, it, half)
                for half in both:
                    a, z = HALVES[half]
                    if kind == "conv1":
                        act.wait_ge(rows_ready[half], before(it))
                        act.wait_ge(y_ready[half], it + 1)
                        nc.scalar.activation(h[:, a:z, :], y[:, a:z, :], ACT.Relu).then_inc(h_ready[half], 1)
                    elif kind != "hop":
                        act.wait_ge(rows_ready[half], before(it))
                        if kind == "conv3":
                            act.wait_ge(stored[half], it * 16 + 16)
                        hold(act, env, norm.factors[half], it + 1)
                        if kind == "last":
                            ins = norm.apply(half, lambda b: den_block(it, b), lambda b: h[:, b, :], ACT.Identity)
                        else:
                            ins = norm.apply(half, lambda b: x_block(it, b), lambda b: h[:, b, :], ACT.Relu)
                        ins.then_inc(h_ready[half], 1)
                if skewed and not last:
                    for half in both:
                        norm.take_root(act, it + 1, half)
                if kind == "conv3":
                    for half in both:
                        norm2.take_root(act, it, half)
                    for half in both:
                        act.wait_ge(norm2.factors[half], it + 1)
                        norm2.apply(half, lambda b: h[:, b, :], lambda b: outrow[:, b, :], ACT.Identity
                                        ).then_inc(y_ready[half], 1)
                if refill:
                    for half in both:
                        a, z = cols(half)
                        hold(act, env, flipped[half], now(it))
                        nc.scalar.copy(env.acc[:, bass.ds(it * BW + a, z - a)], flip[:, a:z]).then_inc(refilled[half], 1)
            turns(act, NTURNS, body)

        steps = 2 * {"start": 3, "conv1": 1, "conv2": 6, "attend": 4, "conv3": 10, "hop": 0, "last": 6}[kind]

        @block.vector
        def _(dve):
            V = nc.vector
            for half in both:
                for s in (product_taken, rows_ready, feat_taken):
                    dve.sem_inc(s[half], 1)
            def program_of(it, link):

                def views(half):
                    a, z = HALVES[half]
                    n = z - a
                    x_half = env.X[:, bass.ds(it * BG + a, n), :]
                    h_half = env.den[:, bass.ds(it * BW + a * P, n * P)].rearrange("p (b f) -> p b f", b=n)
                    return a, z, n, x_half, h_half

                def per_node(values, n):
                    return values.to_broadcast([P, n, F])

                def dis(a, n):
                    return per_node(env.dis[:, bass.ds(it * BG + a, n), factor:factor + 1], n)

                def row(name, n):
                    return env.rows[:, env.row_names.index(name), :].unsqueeze(1).to_broadcast([P, n, F])

                def take_in(half):
                    a, z, n, x_half, h_half = views(half)
                    y_half = y[:, a:z, :]
                    if not skewed:
                        hold(dve, env, rows_ready[half], before(it))
                    elif not (isinstance(it, int) and it == 0):
                        hold(dve, env, norm.factors[half], it)
                    if take:
                        if kind == "hop":
                            dve.wait_ge(stored[half], it * 16 + 16)
                        hold(dve, env, product_ready[half], now(it))
                        lo, hi = cols(half)
                        products = prod[:, lo:hi]
                        prod_rows = products.rearrange("p (b f) -> p b f", b=n)
                        if kind in ("hop", "last"):
                            to = outrow[:, a:z, :] if kind == "hop" else h_half
                            ins = V.scalar_tensor_tensor(
                                out=to.rearrange("p b f -> p (b f)"),
                                in0=env.SC[:, bass.ds(it * BW + lo, hi - lo)], scalar=ALPHA, in1=products,
                                op0=ALU.mult, op1=ALU.add)
                            if kind == "hop":
                                ins.then_inc(rows_ready[half], 1)
                                return
                            link(ins)
                        elif kind == "attend":
                            link(V.tensor_tensor(x_half, x_half, prod_rows, ALU.add))
                        else:
                            link(V.tensor_tensor(y_half, prod_rows, dis(a, n), ALU.mult))
                        dve.sem_inc(product_taken[half], 1)
                        if kind == "conv1":
                            V.tensor_tensor(y_half, y_half, row("L0_gnn_b1", n), ALU.add).then_inc(y_ready[half], 1)
                        elif bias is not None:
                            link(V.tensor_tensor(y_half, y_half, row(env.row_names[bias], n), ALU.add))
                        if kind in ("conv2", "conv3"):
                            link(V.tensor_tensor(x_half, x_half, y_half, ALU.add))
                    if kind in ("start", "conv2", "attend", "conv3"):
                        norm.take_moments(half, lambda b: x_block(it, b), link)
                    elif kind == "last":
                        hold(dve, env, feat_loaded[half], it * 16 + 16)
                        link(V.tensor_tensor(h_half, h_half, feat[:, a:z, :], ALU.add))
                        dve.sem_inc(feat_taken[half], 1)
                        V.tensor_tensor(x_half, x_half, h_half, ALU.add)
                        norm.take_moments(half, lambda b: den_block(it, b), link)

                def give(half):
                    a, z, n, x_half, h_half = views(half)
                    if kind == "conv3":
                        dve.wait_ge(y_ready[half], it + 1)
                        link(V.tensor_tensor(outrow[:, a:z, :], outrow[:, a:z, :], row("L3_gnn_ln1_g", n), ALU.mult))
                        V.tensor_tensor(h_half, outrow[:, a:z, :], row("L3_gnn_ln1_b", n), ALU.add
                                        ).then_inc(rows_ready[half], 1)
                        return
                    hold(dve, env, h_ready[half], it + 1)
                    if refill:
                        dve.wait_ge(stored[half], it * 16 + 16)
                        hold(dve, env, flipped[half], before(it))
                        V.tensor_tensor(outrow[:, a:z, :], h[:, a:z, :], dis(a, n), ALU.mult
                                        ).then_inc(rows_ready[half], 1)
                    elif kind == "conv2":
                        V.tensor_copy(h_half, h[:, a:z, :]).then_inc(rows_ready[half], 1)
                    elif kind == "last":
                        link(V.tensor_tensor(h[:, a:z, :], h[:, a:z, :], row("L3_gnn_ln2_g", n), ALU.mult))
                        V.tensor_tensor(h_half, h[:, a:z, :], row("L3_gnn_ln2_b", n), ALU.add
                                        ).then_inc(rows_ready[half], 1)

                return take_in, give

            def body(it, last):
                link = Links(dve, env, chain, it, steps, ahead_steps)
                take_in, give = program_of(it, link)
                if not skewed:
                    for half in both:
                        take_in(half)
                if normed:
                    for half in both:
                        norm.make_factors(dve, it, half, link)
                if skewed and not last:
                    for half in both:
                        program_of(it + 1, link)[0](half)
                if kind == "conv3":
                    for half in both:
                        hold(dve, env, h_ready[half], it + 1)
                        norm2.take_moments(half, lambda b: h[:, b, :], link)
                    for half in both:
                        norm2.make_factors(dve, it, half, link)
                if kind != "hop":
                    for half in both:
                        give(half)
                if not (skewed and last):
                    link.close()

            ahead_steps = 0
            if skewed:
                ahead = Links(dve, env, chain, 0, steps)
                for half in both:
                    program_of(0, ahead)[0](half)
                ahead_steps = ahead.n
            turns(dve, NTURNS, body)


def project_phase(nc, env, kind):
    with ExitStack() as ctx:
        tag = env.tag(ctx)

        def sb(name, shape, dt=F32):
            return ctx.enter_context(nc.sbuf_tensor(name + tag, shape, dt))

        def sem(name):
            return env.semaphore(name + tag)

        att = kind == "attention"
        nm = NTYPES if att else 1
        ncol = 3 * F if att else 2 * FG + F
        masked = sb("masked", [P, 2, nm, F])
        mT = sb("mT", [P, 2, nm, P])
        outc = sb("outc", [P, 2, ncol])
        weights = (sb("WQKV", [P, NTYPES, 3 * F]), sb("WE", [P, ETYPES, F]), sb("mu", [P, ETYPES])) if att else None
        kT = sb("kT", [P, 2, P]) if att else None
        kv = sb("kv", [P, 2, ETYPES, 2 * F]) if att else None
        flip = ctx.enter_context(nc.psum_tensor("flip" + tag, [P, 2, 512], F32))
        proj = ctx.enter_context(nc.psum_tensor("proj" + tag, [P, 2, 512], F32))
        kflip = ctx.enter_context(nc.psum_tensor("kflip" + tag, [P, 2, 512], F32))
        kproj = ctx.enter_context(nc.psum_tensor("kproj" + tag, [P, 2 * 512], F32))
        (weights_loaded, weights_ready, masked_ready, flipped, turned, projected, copied, key_flipped, key_turned,
         key_projected, v_ready, keys_ready) = (sem(n) for n in (
             "weights_loaded", "weights_ready", "masked_ready", "flipped", "turned", "projected", "copied",
             "key_flipped", "key_turned", "key_projected", "v_ready", "keys_ready"))
        stored = [sem("stored_even"), sem("stored_odd")]
        q_stored = [sem("q_stored_even"), sem("q_stored_odd")]
        block = ctx.enter_context(nc.Block())
        LAG = 2 if att else 1
        per_block = 16 * (1 if att else 3)
        if att:
            WQKV, WE, mu = weights

        def steps(engine, step):
            def at(pair, odd, n):
                def stage_of(back):
                    if n is not None and not 0 <= n - back < NB:
                        return None
                    parity = (odd + back) % 2
                    half = pair + (odd - back - parity) // 2
                    return 2 * half + parity, half, parity
                return stage_of

            first, last = 2, (NB - 1) // 2
            for n in range(-1, 2 * first):
                step(at(n // 2, n % 2, n))
            with engine.Fori(first, last) as pair:
                for odd in range(2):
                    step(at(pair, odd, None))
            for n in range(2 * last, NB + LAG):
                step(at(n // 2, n % 2, n))

        def after(engine, semaphore, count):
            if not (isinstance(count, int) and count <= 0):
                engine.wait_ge(semaphore, count)

        @block.sync
        def _(sp):
            if att:
                for k, name in enumerate(("L1_gnn_W_Q", "L1_gnn_W_K", "L1_gnn_W_V")):
                    sp.dma_start(WQKV[:, :, k * F:(k + 1) * F], env.ins[name].rearrange("t i o -> i t o")
                                 ).then_inc(weights_loaded, 16)
                sp.dma_start(WE[:, :, :], env.ins["L1_gnn_W_edge"].rearrange("t i o -> i t o")
                             ).then_inc(weights_loaded, 16)
                sp.dma_start(mu[:, :], env.ins["L1_gnn_mu"].unsqueeze(0).to_broadcast([P, ETYPES])
                             ).then_inc(weights_loaded, 16)

            def step(stage_of):
                if att and (b := stage_of(1)):
                    n, half, s = b
                    sp.wait_ge(copied, n + 1)
                    sp.dma_start(env.Qtab[bass.ds(n * P, P), :], outc[:, s, 0:F]).then_inc(q_stored[s], 16)
                if b := stage_of(LAG):
                    n, half, s = b
                    rows = bass.ds(n * P, P)
                    sp.wait_ge(keys_ready, n + 1)
                    if att:
                        sp.wait_ge(v_ready, n + 1)
                        sp.dma_start(env.Ktab[rows, :], kv[:, s, :, :].rearrange("p t f -> p (t f)")
                                     ).then_inc(stored[s], 16)
                    else:
                        sp.dma_start(env.FTtab[rows, 0:FG], outc[:, s, 0:FG]).then_inc(stored[s], 16)
                        sp.dma_start(env.FTtab[rows, FG:FG + F], outc[:, s, 2 * FG:2 * FG + F]).then_inc(stored[s], 16)
                        sp.dma_start(env.Dtab[rows, :], outc[:, s, FG:2 * FG]).then_inc(stored[s], 16)
            steps(sp, step)
            sp.wait_ge(stored[0], per_block * (NB // 2 + 1))
            sp.wait_ge(stored[1], per_block * (NB // 2))
            if att:
                sp.wait_ge(q_stored[0], 16 * (NB // 2 + 1))
                sp.wait_ge(q_stored[1], 16 * (NB // 2))

        @block.tensor
        def _(pe):
            if att:
                pe.wait_ge(weights_ready, 1)

            def step(stage_of):
                if b := stage_of(0):
                    n, half, s = b
                    after(pe, turned, n - 1)
                    pe.wait_ge(masked_ready, n + 1)
                    for m in range(nm):
                        ins = nc.tensor.transpose(flip[:, s, m * P:(m + 1) * P], masked[:, s, m, :], env.ident[:, :])
                    ins.then_inc(flipped, 1)
                if att and (b := stage_of(2)):
                    n, half, s = b
                    after(pe, key_turned, n - 1)
                    pe.wait_ge(copied, n + 1)
                    nc.tensor.transpose(kflip[:, s, 0:P], outc[:, s, F:2 * F], env.ident[:, :]
                                        ).then_inc(key_flipped, 1)
                if b := stage_of(1):
                    n, half, s = b
                    after(pe, copied, n - 1)
                    pe.wait_ge(turned, n + 1)
                    for m in range(nm):
                        ins = nc.tensor.matmul(proj[:, s, 0:ncol], lhsT=mT[:, s, m, :],
                                               rhs=WQKV[:, m, :] if att else env.W3[:, :], start=m == 0,
                                               stop=m == nm - 1)
                    ins.then_inc(projected, 1)
                if att and (b := stage_of(2)):
                    n, half, s = b
                    after(pe, keys_ready, n)
                    pe.wait_ge(key_turned, n + 1)
                    for k in range(2):
                        types = WE[:, k * 4:k * 4 + 4, :].rearrange("p t f -> p (t f)")
                        ins = nc.tensor.matmul(kproj[:, k * 512:k * 512 + 512], lhsT=kT[:, s, :], rhs=types,
                                               start=True, stop=True)
                    ins.then_inc(key_projected, 1)
            steps(pe, step)

        @block.vector
        def _(dve):
            if att:
                dve.wait_ge(weights_loaded, 16 * 5)
                nc.vector.tensor_scalar(mu[:, :], mu[:, :], float(F) ** -0.5, None, ALU.mult
                                        ).then_inc(weights_ready, 1)
                dve.wait_ge(weights_ready, 1)
                nc.vector.tensor_tensor(WE[:, :, :], WE[:, :, :], mu[:, :].unsqueeze(2).to_broadcast([P, ETYPES, F]),
                                        ALU.mult).then_inc(weights_ready, 1)

            def step(stage_of):
                if b := stage_of(-1):
                    n, half, s = b
                    after(dve, flipped, n - 1)
                    h_block = env.den[:, bass.ds(n * P, P)]
                    if att:
                        kinds = env.nmask[:, bass.ds(n, 1), :].rearrange("p a t -> p (a t)")
                        nc.vector.tensor_tensor(masked[:, s, :, :], h_block.unsqueeze(1).to_broadcast([P, NTYPES, F]),
                                                kinds.unsqueeze(2).to_broadcast([P, NTYPES, F]), ALU.mult
                                                ).then_inc(masked_ready, 1)
                    else:
                        nc.vector.tensor_copy(masked[:, s, 0, :], h_block).then_inc(masked_ready, 1)
                if not att and (b := stage_of(1)):
                    n, half, s = b
                    dve.wait_ge(copied, n + 1)
                    tail = outc[:, s, FG:FG + F]
                    nc.vector.tensor_scalar(tail, tail, env.logdeg[:, bass.ds(n, 1)], None, ALU.mult
                                            ).then_inc(keys_ready, 1)
                if att and (b := stage_of(2)):
                    n, half, s = b
                    dve.wait_ge(key_flipped, n + 1)
                    nc.vector.tensor_copy(kT[:, s, :], kflip[:, s, 0:P]).then_inc(key_turned, 1)
                    after(dve, stored[s], per_block * half)
                    dve.wait_ge(key_projected, n + 1)
                    nc.vector.tensor_copy(kv[:, s, :, 0:F], kproj[:, :].rearrange("p (t f) -> p t f", t=ETYPES)
                                          ).then_inc(keys_ready, 1)
            steps(dve, step)

        @block.scalar
        def _(act):
            def step(stage_of):
                if b := stage_of(0):
                    n, half, s = b
                    after(act, projected, n - 1)
                    act.wait_ge(flipped, n + 1)
                    nc.scalar.copy(mT[:, s, :, :].rearrange("p m f -> p (m f)"), flip[:, s, 0:nm * P]
                                   ).then_inc(turned, 1)
                if b := stage_of(1):
                    n, half, s = b
                    if att:
                        after(act, q_stored[s], 16 * half)
                        after(act, key_flipped, n - 1)
                        after(act, v_ready, n - 1)
                    else:
                        after(act, stored[s], per_block * half)
                    act.wait_ge(projected, n + 1)
                    nc.scalar.copy(outc[:, s, :], proj[:, s, 0:ncol]).then_inc(copied, 1)
                if att and (b := stage_of(2)):
                    n, half, s = b
                    after(act, stored[s], per_block * half)
                    act.wait_ge(copied, n + 1)
                    v_row = outc[:, s, 2 * F:3 * F].unsqueeze(1).to_broadcast([P, ETYPES, F])
                    nc.scalar.copy(kv[:, s, :, F:2 * F], v_row).then_inc(v_ready, 1)
            steps(act, step)


def feed_forward_phase(nc, env, out):
    with ExitStack() as ctx:
        tag = env.tag(ctx)

        def sb(name, shape, dt=F32):
            return ctx.enter_context(nc.sbuf_tensor(name + tag, shape, dt))

        def sem(name):
            return env.semaphore(name + tag)

        NC = FF // P
        FW1, FW2, fb1 = sb("FW1", [P, FF]), sb("FW2", [P, NC, F]), sb("fb1", [P, NC])
        h = sb("h", [P, BG, F])
        hT = sb("hT", [P, BW])
        hidden = sb("hidden", [P, NC, BW])
        y = sb("y", [P, BG, F])
        flip = ctx.enter_context(nc.psum_tensor("flip" + tag, [P, 2 * 512], F32))
        up = ctx.enter_context(nc.psum_tensor("up" + tag, [P, 2, 2 * 512], F32))
        down = ctx.enter_context(nc.psum_tensor("down" + tag, [P, 2 * 512], F32))
        weights_loaded = sem("weights_loaded")
        taken, flipped, turned, up_ready, relued, y_ready = (
            sem(n) for n in ("taken", "flipped", "turned", "up_ready", "relued", "y_ready"))
        down_ready, biased, stored = (sem(n) for n in ("down_ready", "biased", "stored"))
        block = ctx.enter_context(nc.Block())

        @block.sync
        def _(sp):
            sp.sem_inc(stored, 16)
            for dst_, src_ in ((FW1[:, :], env.ins["L3_W1T"]), (fb1[:, :], env.ins["L3_b1"]),
                               (FW2[:, :, :], env.ins["L3_W2T"].rearrange("(c p) o -> p c o", p=P))):
                sp.dma_start(dst_, src_).then_inc(weights_loaded, 16)
            with sp.Fori(0, NTURNS - 1) as it:
                sp.wait_ge(y_ready, it + 1)
                sp.dma_start(out[bass.ds(it * BW, BW), :].rearrange("(b p) f -> p b f", p=P), y[:, :, :]
                             ).then_inc(stored, 16)
            sp.wait_ge(y_ready, NTURNS)
            first = (NTURNS - 1) * BW
            full = (N_NODES - first) // P
            rest = N_NODES - first - full * P
            sp.dma_start(out[first:first + full * P, :].rearrange("(b p) f -> p b f", p=P), y[:, 0:full, :]
                         ).then_inc(stored, 16)
            sp.dma_start(out[first + full * P:N_NODES, :], y[0:rest, full, :]).then_inc(stored, 16)
            sp.wait_ge(stored, 16 * (NTURNS + 2))

        @block.tensor
        def _(pe):
            pe.wait_ge(weights_loaded, 48)
            pe.sem_inc(down_ready, 1)

            def turn_rows(it):
                pe.wait_ge(taken, it + 1)
                for b in range(BG):
                    ins = nc.tensor.transpose(flip[:, b * P:(b + 1) * P], h[:, b, :], env.ident[:, :])
                ins.then_inc(flipped, 1)

            def multiply(it, last):
                pe.wait_ge(turned, it + 1)
                for c in range(NC):
                    if c >= 2:
                        pe.wait_ge(relued, it * NC + c - 1)
                    for a, b in ((0, 512), (512, BW)):
                        ins = nc.tensor.matmul(up[:, c % 2, a:b], lhsT=FW1[:, c * P:(c + 1) * P], rhs=hT[:, a:b],
                                               start=True, stop=True)
                    ins.then_inc(up_ready, 1)
                if not last:
                    turn_rows(it + 1)
                pe.wait_ge(relued, it * NC + NC)
                pe.wait_ge(biased, it + 1)
                for b in range(BG):
                    for c in range(NC):
                        ins = nc.tensor.matmul(down[:, b * P:(b + 1) * P], lhsT=hidden[:, c, b * P:(b + 1) * P],
                                               rhs=FW2[:, c, :], start=c == 0, stop=c == NC - 1)
                ins.then_inc(down_ready, 1)

            turn_rows(0)
            turns(pe, NTURNS, multiply)

        @block.scalar
        def _(act):
            act.wait_ge(weights_loaded, 48)
            with act.Fori(0, NTURNS) as it:
                act.wait_ge(flipped, it + 1)
                nc.scalar.copy(hT[:, :], flip[:, 0:BW]).then_inc(turned, 1)
                act.wait_ge(down_ready, it + 1)
                for c in range(NC):
                    act.wait_ge(up_ready, it * NC + c + 1)
                    nc.scalar.activation(hidden[:, c, :], up[:, c % 2, 0:BW], ACT.Relu, bias=fb1[:, c:c + 1]
                                         ).then_inc(relued, 1)

        @block.vector
        def _(dve):
            dve.sem_inc(biased, 1)

            def take_rows(it):
                nc.vector.tensor_copy(h[:, :, :], env.den[:, bass.ds(it * BW, BW)].rearrange(
                    "p (b f) -> p b f", b=BG)).then_inc(taken, 1)

            def finish(it, last):
                if not last:
                    hold(dve, env, flipped, it + 1)
                    take_rows(it + 1)
                dve.wait_ge(stored, it * 16 + 16)
                dve.wait_ge(down_ready, it + 2)
                b2 = env.rows[:, env.row_names.index("L3_gnn_b2"), :].unsqueeze(1).to_broadcast([P, BG, F])
                nc.vector.tensor_tensor(y[:, :, :], down[:, 0:BW].rearrange("p (b f) -> p b f", b=BG), b2, ALU.add
                                        ).then_inc(biased, 1)
                dve.wait_ge(biased, it + 2)
                nc.vector.tensor_tensor(y[:, :, :], y[:, :, :], env.X[:, bass.ds(it * BG, BG), :], ALU.add
                                        ).then_inc(y_ready, 1)

            take_rows(0)
            turns(dve, NTURNS, finish)


def program(nc, ins, out):
    env = Env()
    env.nc = nc
    env.ins = ins
    env.src_groups = ins["src_groups"]
    with ExitStack() as ctx:
        def sb(name, shape, dt=F32):
            return ctx.enter_context(nc.sbuf_tensor(name, shape, dt))

        def dram(name, shape, dt=F32):
            return nc.dram_tensor(name, shape, dt, kind="Internal").ap()

        env.held = ctx.enter_context(nc.semaphore("held"))
        env.X = sb("X", [P, NB, F])
        env.acc = sb("acc", [P, HEADS * NTR])
        env.den = sb("den", [P, HEADS * NTR])
        env.SC = sb("SC", [P, HEADS * NTR])
        env.W = sb("W", [P, HEADS * NTR])
        env.eweight = sb("eweight", [P, NTX])
        env.dloc = sb("dloc", [P, NTX])
        env.starts = sb("starts", [1, NTX], I32)
        env.rowdstf = sb("rowdstf", [P, RB, P])
        env.iota = sb("iota", [P, P])
        env.ident = sb("ident", [P, P])
        env.dis = sb("dis", [P, NB, 2])
        env.logdeg = sb("logdeg", [P, NB])
        env.nmask = sb("nmask", [P, NB, NTYPES])
        env.L0W1, env.L0W2, env.L2W = sb("L0W1", [P, F]), sb("L0W2", [P, F]), sb("L2W", [P, F])
        env.W3 = sb("W3", [P, 2 * FG + F])
        env.row_names = ["L0_gnn_b1", "L0_gnn_b2", "L2_gnn_bias", "L3_gnn_ln1_g", "L3_gnn_ln1_b", "L3_gnn_ln2_g",
                         "L3_gnn_ln2_b", "L3_gnn_b2"]
        env.rows = sb("rows_b", [P, len(env.row_names), F])
        env.kidx_groups = dram("kidx_groups", [NG, P, GT], I32)
        env.Htab = dram("Htab", [NPAD, F])
        env.Ktab = dram("Ktab", [NPAD, ETYPES * 2 * F])
        env.kept = dram("kept", [NG, P, GT * F])
        env.Qtab = dram("Qtab", [NWIN, F])
        env.FTtab = dram("FTtab", [NPAD, FG + F])
        env.Dtab = dram("Dtab", [NWIN, FG])
        env.Ftab = dram("Ftab", [NPAD, F])
        env.Feat = dram("Feat", [NPAD, F])
        env.edge_scale = env.eweight

        load_phase(nc, env)
        degrees_phases(nc, env)
        node_phase(nc, env, "start")
        aggregate_phase(nc, env, env.Htab, None, "edge", None, False)
        node_phase(nc, env, "conv1")
        aggregate_phase(nc, env, env.Htab, None, "edge", None, False)
        node_phase(nc, env, "conv2")
        project_phase(nc, env, "attention")
        keys = env.Ktab.rearrange("n (t f) -> (n t) f", t=ETYPES)
        score_phase(nc, env, keys, env.kidx_groups, env.Qtab, env.kept, 1, F)
        softmax_phase(nc, env, 1, -1e9, 1e-10, 1.0, False)
        env.edge_scale = env.W
        aggregate_phase(nc, env, None, env.kept, "edge", None, True)
        node_phase(nc, env, "attend")
        aggregate_phase(nc, env, env.Htab, None, None, None, False)
        node_phase(nc, env, "conv3")
        project_phase(nc, env, "diffusion")
        score_phase(nc, env, env.FTtab, env.src_groups, env.Dtab, env.kept, HEADS, FG)
        softmax_phase(nc, env, HEADS, None, 0.0, 1.0 - ALPHA, True)
        f0 = (env.SC[:, 0:NPAD].rearrange("p (b f) -> p b f", b=NB),
              env.FTtab[:, FG:FG + F].rearrange("(b p) f -> p b f", p=P))
        aggregate_phase(nc, env, None, env.kept, "heads", None, True, beside=f0)
        for hop in range(HOPS - 1):
            node_phase(nc, env, "hop")
            aggregate_phase(nc, env, env.Ftab, None, "heads", None, True)
        node_phase(nc, env, "last")
        feed_forward_phase(nc, env, out)


def kernel(**inputs):
    import numpy as np
    import concourse.bacc as bacc
    from concourse.bass_utils import run_bass_kernel_spmd as run

    given = {k: np.asarray(v) for k, v in inputs.items()}

    def padded(a, n, value=0):
        return np.concatenate([a, np.full((n - a.shape[0], *a.shape[1:]), value, a.dtype)])

    def grouped(a):
        return np.ascontiguousarray(padded(a, NT * P).reshape(NG, GT, P).transpose(0, 2, 1))

    dst = padded(given["dst"], NTR * P, PAD_NODE)
    by_row = dst.reshape(NTR, P)
    arrays = {
        "x": padded(given["x"], NPAD),
        "src_groups": grouped(given["src"]),
        "etype_groups": grouped(given["edge_type_8"]),
        "eweight": np.ascontiguousarray(padded(given["edge_weight"], NT * P).reshape(NT, P).T),
        "dst_tiles": np.ascontiguousarray(by_row[:NT].T),
        "starts": np.ascontiguousarray(by_row[:NT, 0].reshape(1, NT)),
        "dst_rows": np.ascontiguousarray(by_row.reshape(RB, P, P).transpose(1, 0, 2)),
        "dst_ends": np.ascontiguousarray(by_row[:, [0, P - 1]].T),
        "ntype": np.ascontiguousarray(padded(given["node_type_4"], NPAD).reshape(NB, P).T),
        "L2_WT": np.ascontiguousarray(given["L2_gnn_weight"].T),
        "L3_WhT": np.ascontiguousarray(given["L3_gnn_Wh"].T),
        "L3_WtT": np.ascontiguousarray(given["L3_gnn_Wt"].T),
        "L3_WeT": np.ascontiguousarray(given["L3_gnn_We"].T),
        "L3_W1T": np.ascontiguousarray(given["L3_gnn_W1"].T),
        "L3_W2T": np.ascontiguousarray(given["L3_gnn_W2"].T),
        "L3_b1": np.ascontiguousarray(given["L3_gnn_b1"].reshape(FF // P, P).T),
        "L3_attn": given["L3_gnn_attn_p"].reshape(F),
        "L3_ghead": given["L3_gnn_g_head"].reshape(F),
        "L3_gtail": given["L3_gnn_g_tail"].reshape(F),
    }
    for name in ("L0_gnn_W1", "L0_gnn_W2", "L1_gnn_W_Q", "L1_gnn_W_K", "L1_gnn_W_V", "L1_gnn_W_edge", "L1_gnn_mu",
                 "L0_gnn_b1", "L0_gnn_b2", "L2_gnn_bias", "L3_gnn_ln1_g", "L3_gnn_ln1_b", "L3_gnn_ln2_g",
                 "L3_gnn_ln2_b", "L3_gnn_b2"):
        arrays[name] = np.ascontiguousarray(given[name])

    nc = bacc.Bacc("TRN2", target_bir_lowering=False, num_devices=1)
    ins = {k: nc.dram_tensor(f"in_{k}", v.shape, mybir.dt.from_np(v.dtype), kind="ExternalInput").ap()
           for k, v in arrays.items()}
    out = nc.dram_tensor("out", (N_NODES, F), F32, kind="ExternalOutput").ap()
    program(nc, ins, out)
    result = run(nc, [{f"in_{k}": v for k, v in arrays.items()}], core_ids=[0])
    return result.results[0]["out"]
```
